# Optimizing a Trainium2 kernel written in Bass

```python
import numpy as np
import jax
import jax.numpy as jnp

def _softmax(x, axis=-1):
    return jax.nn.softmax(x, axis=axis)

def _gelu(x):
    return jax.nn.gelu(x, approximate=True)

def _silu(x):
    return jax.nn.silu(x)

def _sigmoid(x):
    return jax.nn.sigmoid(x)

def _layernorm(x, axis=-1, eps=1e-05):
    m = jnp.mean(x, axis=axis, keepdims=True)
    v = jnp.var(x, axis=axis, keepdims=True)
    return (x - m) / jnp.sqrt(v + eps)

def _scatter_add(tgt, idx, src, axis=0):
    return tgt.at[idx].add(src)

def _segment_sum(src, seg, n):
    return jax.ops.segment_sum(src, seg, n)
kernel_name = 'mk_hybrid_d1_jaxref_r4_d95e26'

def setup_inputs(seed: int=0):
    np.random.seed(seed)
    _w = jnp.asarray

    def _L0_attn_a_setup():
        import jax, jax.numpy as jnp
        import numpy as np
        HEAD_NUM = 16
        NEG_BIG = 1000000.0
        key = jax.random.key(seed)
        ks = jax.random.split(key, 5)
        E = 256
        B, S = (1, 1024)
        x = jax.random.normal(ks[0], (B, S, E), dtype=jnp.float32)
        W1 = jax.random.normal(ks[1], (E, 3 * E), dtype=jnp.float32) * (1.0 / np.sqrt(E))
        b1 = jax.random.normal(ks[2], (3 * E,), dtype=jnp.float32) * 0.02
        Wp = jax.random.normal(ks[3], (E, E), dtype=jnp.float32) * (1.0 / np.sqrt(E))
        bp = jax.random.normal(ks[4], (E,), dtype=jnp.float32) * 0.02
        return {'x': x, 'W1': W1, 'b1': b1, 'Wp': Wp, 'bp': bp}
    _L0_attn_a_in = _L0_attn_a_setup()

    def _L0_attn_b_setup():
        import jax, jax.numpy as jnp
        import numpy as np
        B, L, D, H, W = (2, 256, 256, 16, 64)
        DH = D // H
        key = jax.random.key(seed)
        ks = jax.random.split(key, 7)
        scale = 0.02
        return {'x': jax.random.normal(ks[0], (B, L, D), dtype=jnp.float32), 'Wq': jax.random.normal(ks[1], (D, D), dtype=jnp.float32) * scale, 'Wk': jax.random.normal(ks[2], (D, D), dtype=jnp.float32) * scale, 'Wv': jax.random.normal(ks[3], (D, D), dtype=jnp.float32) * scale, 'Wo': jax.random.normal(ks[4], (D, D), dtype=jnp.float32) * scale, 'last_k_init': jax.random.normal(ks[5], (W - 1, H, DH), dtype=jnp.float32), 'last_v_init': jax.random.normal(ks[6], (W - 1, H, DH), dtype=jnp.float32)}
    _L0_attn_b_in = _L0_attn_b_setup()

    def _L0_ffn_setup():
        import jax, jax.numpy as jnp
        import numpy as np
        DIM = 256
        HIDDEN = 768
        SCALE = 1.0 / 127.0

        def _dequant(w_int, dtype):
            return w_int.astype(dtype) * jnp.asarray(SCALE, dtype)
        key = jax.random.key(seed)
        k_x, k_g, k_u, k_d = jax.random.split(key, 4)
        x = jax.random.normal(k_x, (4, 512, DIM), dtype=jnp.float32)
        w_gate = jax.random.randint(k_g, (HIDDEN, DIM), -127, 128, dtype=jnp.int32)
        w_up = jax.random.randint(k_u, (HIDDEN, DIM), -127, 128, dtype=jnp.int32)
        w_down = jax.random.randint(k_d, (DIM, HIDDEN), -127, 128, dtype=jnp.int32)
        return {'x': x, 'w_gate': w_gate, 'w_up': w_up, 'w_down': w_down}
    _L0_ffn_in = _L0_ffn_setup()
    _d = {'L0_attn_a_x': _L0_attn_a_in['x'], 'L0_attn_a_W1': _L0_attn_a_in['W1'], 'L0_attn_a_b1': _L0_attn_a_in['b1'], 'L0_attn_a_Wp': _L0_attn_a_in['Wp'], 'L0_attn_a_bp': _L0_attn_a_in['bp'], 'L0_attn_b_Wq': _L0_attn_b_in['Wq'], 'L0_attn_b_Wk': _L0_attn_b_in['Wk'], 'L0_attn_b_Wv': _L0_attn_b_in['Wv'], 'L0_attn_b_Wo': _L0_attn_b_in['Wo'], 'L0_attn_b_last_k_init': _L0_attn_b_in['last_k_init'], 'L0_attn_b_last_v_init': _L0_attn_b_in['last_v_init'], 'L0_ffn_w_gate': _L0_ffn_in['w_gate'], 'L0_ffn_w_up': _L0_ffn_in['w_up'], 'L0_ffn_w_down': _L0_ffn_in['w_down']}
    _x0 = _d['L0_attn_a_x']
    _d['L0_attn_a_x'] = jax.random.normal(jax.random.fold_in(jax.random.key(seed), 1), (4, 1024, 256), dtype=_x0.dtype)
    del _x0
    return _d

def reference(L0_attn_a_x, L0_attn_a_W1, L0_attn_a_b1, L0_attn_a_Wp, L0_attn_a_bp, L0_attn_b_Wq, L0_attn_b_Wk, L0_attn_b_Wv, L0_attn_b_Wo, L0_attn_b_last_k_init, L0_attn_b_last_v_init, L0_ffn_w_gate, L0_ffn_w_up, L0_ffn_w_down):

    def _L0_attn_a_ref(x, W1, b1, Wp, bp):
        import jax, jax.numpy as jnp
        import numpy as np
        HEAD_NUM = 16
        NEG_BIG = 1000000.0
        B, S, E = x.shape
        H = HEAD_NUM
        d = E // H
        dk = jnp.asarray(d, x.dtype) ** 0.5
        h = x @ W1 + b1
        h = jnp.swapaxes(h.reshape(B, S, H, 3 * d), 1, 2)
        q, k, v = (h[..., :d], h[..., d:2 * d], h[..., 2 * d:])
        w = jnp.einsum('bhqd,bhkd->bhqk', q, k) / dk
        mask = jnp.tril(jnp.ones((S, S), dtype=x.dtype))
        w = jax.nn.softmax(w * mask - (1.0 - mask) * NEG_BIG, axis=-1)
        a = jnp.einsum('bhqk,bhkd->bhqd', w, v)
        a = jnp.swapaxes(a, 1, 2).reshape(B, S, E)
        return a @ Wp + bp

    def _L0_attn_b_ref(x, Wq, Wk, Wv, Wo, last_k_init, last_v_init):
        import jax, jax.numpy as jnp
        import numpy as np
        B, L, D, H, W = (2, 256, 256, 16, 64)
        DH = D // H
        b, l, d = x.shape
        w1, h, dh = last_k_init.shape
        w = w1 + 1
        q = (x @ Wq.T).reshape(b, l, h, dh)
        k = (x @ Wk.T).reshape(b, l, h, dh)
        v = (x @ Wv.T).reshape(b, l, h, dh)
        last_k = jnp.broadcast_to(last_k_init[None], (b, w1, h, dh))
        last_v = jnp.broadcast_to(last_v_init[None], (b, w1, h, dh))
        k_pad = jnp.concatenate([last_k, k], axis=1)
        v_pad = jnp.concatenate([last_v, v], axis=1)
        idx = jnp.arange(l)[:, None] + jnp.arange(w)[None, :]
        k_win = k_pad[:, idx]
        v_win = v_pad[:, idx]
        scores = jnp.einsum('blhd,blwhd->blwh', q, k_win) * dh ** (-0.5)
        attn = jax.nn.softmax(scores, axis=2)
        out = jnp.einsum('blwh,blwhd->blhd', attn, v_win).reshape(b, l, d)
        return out @ Wo.T

    def _L0_ffn_ref(x, w_gate, w_up, w_down):
        import jax, jax.numpy as jnp
        import numpy as np
        DIM = 256
        HIDDEN = 768
        SCALE = 1.0 / 127.0

        def _dequant(w_int, dtype):
            return w_int.astype(dtype) * jnp.asarray(SCALE, dtype)
        wg = _dequant(w_gate, x.dtype)
        wu = _dequant(w_up, x.dtype)
        wd = _dequant(w_down, x.dtype)
        gate = jnp.einsum('bsd,hd->bsh', x, wg)
        up = jnp.einsum('bsd,hd->bsh', x, wu)
        h = jax.nn.silu(gate) * up
        return jnp.einsum('bsh,dh->bsd', h, wd)
    x = L0_attn_a_x
    x = x + _L0_attn_a_ref(_layernorm(x, axis=-1), L0_attn_a_W1, L0_attn_a_b1, L0_attn_a_Wp, L0_attn_a_bp)
    x = x + _L0_ffn_ref(_layernorm(x, axis=-1), L0_ffn_w_gate, L0_ffn_w_up, L0_ffn_w_down)
    x = x + _L0_attn_b_ref(_layernorm(x, axis=-1), L0_attn_b_Wq, L0_attn_b_Wk, L0_attn_b_Wv, L0_attn_b_Wo, L0_attn_b_last_k_init, L0_attn_b_last_v_init)
    x = x + _L0_ffn_ref(_layernorm(x, axis=-1), L0_ffn_w_gate, L0_ffn_w_up, L0_ffn_w_down)
    return x

_drawn_inputs = setup_inputs


def setup_inputs(seed=0):
    import zlib

    import numpy as np

    out = dict(_drawn_inputs(seed))
    spreads = {}
    factors = {'L0_attn_b_Wq': 52.493,
     'L0_attn_b_Wk': 64.0,
     'L0_attn_b_Wv': 64.0,
     'L0_attn_b_Wo': 50.801,
     'L0_attn_b_last_k_init': 64.0,
     'L0_attn_b_last_v_init': 64.0}
    for name, (base, spread) in spreads.items():
        noise = np.random.default_rng([zlib.crc32(name.encode()), seed]).standard_normal(out[name].shape)
        drawn = base * np.exp(spread * noise) if base else spread * noise
        out[name] = jnp.asarray(drawn.astype(out[name].dtype))
    for name, factor in factors.items():
        out[name] = (out[name] * factor).astype(out[name].dtype)
    return out
```

```python
from contextlib import ExitStack

import numpy as np

import concourse.bass as bass
from concourse import mybir

P = 128
B, S, E = 4, 1024, 256
HEADS, DH = 16, 16
GROUPS, HG = 4, 4
W = 64
HIDDEN = 768
NT = S // P
HALF = S // 2
KPAD = W + S + W
SP_ROWS = 6 * DH
MAX_ROWS = SP_ROWS + 2
Q_PART = (0, 1, 0, 1, 2, 0)
K_PART = (0, 0, 1, 1, 0, 2)
M_HID = HIDDEN // P
EPS = 1e-5
QSCALE = 0.25
DEQUANT = float(np.float32(1.0 / 127.0))
MASKED = -1.0e30
RING = 3

ALU = mybir.AluOpType
ACT = mybir.ActivationFunctionType
AX = mybir.AxisListType
F32 = mybir.dt.float32
F32R = mybir.dt.float32r
BF16 = mybir.dt.bfloat16
I32 = mybir.dt.int32


class Plan:

    def __init__(self, causal):
        self.causal = causal
        self.n_a = NT * HG if causal else NT
        self.per_j = HG if causal else 1
        self.n_j = NT if causal else NT + 1
        self.n_b = self.n_j * self.per_j
        ev = [("A", 0, k) for k in range(self.n_a)] + [("T", 0, 0)]
        for g in range(GROUPS):
            a = 0
            for p in range(self.n_b):
                ev.append(("B", g, p))
                if g + 1 < GROUPS:
                    if a < self.n_a:
                        upto = min(self.n_a, -(-(p + 1) * self.n_a * 5 // (self.n_b * 4)))
                        ev += [("A", g + 1, k) for k in range(a, upto)]
                        a = upto
                    elif a == self.n_a:
                        ev.append(("T", g + 1, 0))
                        a += 1
                if p % self.per_j == self.per_j - 1 and p >= self.per_j:
                    ev.append(("V", g, p // self.per_j - 1))
            if g + 1 < GROUPS and a == self.n_a:
                ev.append(("T", g + 1, 0))
            ev.append(("V", g, self.n_j - 1))
        self.events = ev
        self.ring = [e for e in ev if e[0] != "V"]
        self.slot = {e: n % RING for n, e in enumerate(self.ring)}
        self.before = {e: self.ring[n - RING] if n >= RING else None for n, e in enumerate(self.ring)}

    def a_tile(self, k):
        return (NT - 1 - k // HG, k % HG) if self.causal else (k, None)

    def b_tile(self, p):
        j = p // self.per_j
        return (NT - 1 - j, p % HG) if self.causal else (j, None)

    def queries(self, j):
        if self.causal:
            return P * j, S
        return max(0, P * j - W), min(S, P * j + P)


PLANS = (Plan(True), Plan(False))
A_BASE = (0, GROUPS * PLANS[0].n_a)
B_BASE = (0, GROUPS * PLANS[0].n_b)
V_BASE = (0, GROUPS * PLANS[0].n_j)
A_ALL = A_BASE[1] + GROUPS * PLANS[1].n_a
B_ALL = B_BASE[1] + GROUPS * PLANS[1].n_b
V_ALL = V_BASE[1] + GROUPS * PLANS[1].n_j
VT = (NT, NT + 1)
VT_BASE = (0, NT)


def layers_kernel(nc, x, att_a, att_b, b_qk, b_v, wp_a, wp_b, b_p, w_gu, w_dn, k_init, v_init, out):
    img_qkv = [nc.dram_tensor(f"img_qkv{a}", [P, 3072], F32, kind="Internal").ap() for a in range(2)]
    img_wp = [nc.dram_tensor(f"img_wp{a}", [P, 2048], F32, kind="Internal").ap() for a in range(2)]
    img_gu = nc.dram_tensor("img_gu", [P, 6144], F32, kind="Internal").ap()
    ones_dram = nc.dram_tensor("ones_dram", [2, HEADS * KPAD], BF16, kind="Internal").ap()

    with ExitStack() as ctx:
        where = [16512]

        def region(size):
            at = where[0]
            where[0] += (size + 31) // 32 * 32
            assert where[0] <= nc.sbuf_usable_end, where[0]
            return at

        def at(name, address, shape, dt):
            return nc.alloc_sbuf_tensor_at(name, shape, dt, offset=address)

        def sb(name, shape, dt):
            n = int(np.prod(shape[1:])) * (2 if dt == BF16 else 4)
            return at(name, region(n), shape, dt)

        def sem(name):
            return ctx.enter_context(nc.semaphore(name))

        ring = ctx.enter_context(nc.psum_tensor("ring", [P, RING, 2, 512], F32))
        opsum = ctx.enter_context(nc.psum_tensor("opsum", [P, 2, 512], F32))

        X = sb("X", [P, NT, E], F32)
        r_xt = region(32768)
        xt_hi = at("xt_hi", r_xt, [P, 2, KPAD], F32R)
        xt_lo = at("xt_lo", r_xt + 2 * KPAD * 4, [P, 2, KPAD], F32R)
        t32 = at("t32", r_xt + 18432, [P, S], F32)
        rest = at("rest", r_xt + 18432 + 4096, [P, 2, S], F32)
        on_hi = at("on_hi", r_xt, [P, GROUPS, S], F32R)
        on_lo = at("on_lo", r_xt + 16384, [P, GROUPS, S], F32R)
        r_z = region(73728)
        q_st = at("q_st", r_z, [MAX_ROWS, HEADS, S], BF16)
        k_st = at("k_st", r_z + HEADS * S * 2, [MAX_ROWS, HEADS, KPAD], BF16)
        h_hi = at("h_hi", r_z, [P, M_HID, S], F32R)
        h_lo = at("h_lo", r_z + 24576, [P, M_HID, S], F32R)
        w_gu_sb = at("w_gu_sb", r_z + 49152, [P, 2, 2, 2 * HIDDEN], F32R)
        raw = [at(f"raw{i}", r_z + 36864 * i, [P, 3072], F32) for i in range(2)]
        raw_i = [at(f"raw_i{i}", r_z + 36864 * i, [P, 3072], I32) for i in range(2)]
        st_hi = [at(f"st_hi{i}", r_z + 36864 * i + 12288, [P, 3072], F32R) for i in range(2)]
        st_lo = [at(f"st_lo{i}", r_z + 36864 * i + 24576, [P, 3072], F32R) for i in range(2)]
        r_p = region(32768)
        probs = at("probs", r_p, [P, 2, HG, S], F32)
        q_part = at("q_part", r_p, [P, 2, 3, S], BF16)
        k_part = at("k_part", r_p + 12288, [P, 2, 3, KPAD], BF16)
        wp_sb = at("wp_sb", r_p, [P, GROUPS, 512], F32R)
        xn = at("xn", r_p + 24576, [P, NT, E], F32)
        gate = at("gate", r_p + 24576, [P, 2, HALF], F32)
        hid = at("hid", r_p + 24576 + 4096, [P, 2, HALF], F32)
        V = sb("V", [P, NT + 1, HEADS, 2 * DH], F32)
        w_qkv = sb("w_qkv", [P, 3072], F32R)
        w_dn_sb = sb("w_dn_sb", [P, M_HID, 512], F32R)
        osb = sb("osb", [P, S], F32)
        onf = sb("onf", [P, S], F32)
        ident = sb("ident", [P, P], F32)
        ident_b = sb("ident_b", [P, P], BF16)
        mask_a = [sb("mask_a0", [P, P], BF16), sb("mask_a1", [P, P + W], BF16)]
        mask_b = [sb("mask_b0", [P, P], BF16), sb("mask_b1", [P, P + W], BF16)]
        peak = sb("peak", [P, 2, 32], F32)
        peak_b = sb("peak_b", [32, 2, P], BF16)
        bias_v = sb("bias_v", [P, 2, E], F32)
        bias_p = sb("bias_p", [P, E], F32)
        bias_qk = sb("bias_qk", [P, 4], F32)
        bias_q4 = sb("bias_q4", [P, 4], F32)
        v_pre = sb("v_pre", [W, E], F32)
        k_pre = sb("k_pre", [P, 2, 3, W], BF16)
        vtmp = sb("vtmp", [P, 2, E], F32)
        stats = sb("stats", [P, NT, 6], F32)
        mv = sb("mv", [P, NT, 2], F32)
        std = sb("std", [P, NT], F32)
        rstd = sb("rstd", [P, NT], F32)
        sums = sb("sums", [P, 32], F32)
        rsum = sb("rsum", [P, 32], F32)
        k_raw = at("k_raw", r_p, [P, 2, W], F32)
        k_res = at("k_res", r_p + 1024, [P, 2, 2, W], F32)
        mask_f = at("mask_f", r_p + 4096, [P, 4, P + W], F32)
        ones_b = at("ones_b", r_p + 8192, [P, 2, 144], BF16)

        s_small = sem("small_loaded")
        s_raw = [sem("raw_loaded0"), sem("raw_loaded1")]
        s_split = sem("weights_split")
        s_img = [sem("image_stored0"), sem("image_stored1")]
        s_pool = sem("pool_setup")
        s_dve = sem("dve_setup")
        s_ones = sem("ones_stored")
        arrived = sem("engines_arrived")
        go_on = {n: sem(f"go_on_{n}") for n in ("pool", "dve", "act", "pe")}

        names = {}
        for n in ("x_in qkv_in wp_in gu_in ones_in pads kpads stats_done aggr_done std_done rstd_done xn_done "
                  "turned xhi_done xlo_done qk_ready qk_evac part_hi part_rest part_mid part_lo stack0 stack1 "
                  "v_ready v_tmp v_done v_pre_set a_ready a_max t_ready peak_hi peak_done peak_rows "
                  "b_ready exp_done pv_done o_copied sums_out rsum_done rsum_back bcast_done on_f on_hi_done "
                  "on_lo_done x_bias proj_ready res_half res_done gu_ready gate_done hid_done h_hi_done "
                  "h_lo_done out_stored").split():
            names[n] = sem(n)
        (x_in, qkv_in, wp_in, gu_in, ones_in, pads, kpads, stats_done, aggr_done, std_done, rstd_done, xn_done,
         turned, xhi_done, xlo_done, qk_ready, qk_evac, part_hi, part_rest, part_mid, part_lo, stack0, stack1,
         v_ready, v_tmp, v_done, v_pre_set, a_ready, a_max, t_ready, peak_hi, peak_done, peak_rows,
         b_ready, exp_done, pv_done, o_copied, sums_out, rsum_done, rsum_back, bcast_done, on_f, on_hi_done,
         on_lo_done, x_bias, proj_ready, res_half, res_done, gu_ready, gate_done, hid_done, h_hi_done,
         h_lo_done, out_stored) = names.values()
        stack_in = (stack0, stack1)
        totals = {
            x_in: 16, qkv_in: 32, wp_in: 32, gu_in: 32, ones_in: 32, pads: 4, kpads: 2,
            stats_done: 4 * NT, aggr_done: 4 * NT, std_done: 4, rstd_done: 4, xn_done: 4 * NT,
            turned: 8, xhi_done: 8, xlo_done: 8,
            qk_ready: 8, qk_evac: 8, part_hi: 8, part_rest: 8, part_mid: 8, part_lo: 8,
            stack0: 2 * 192, stack1: 2 * 192, v_ready: sum(VT), v_tmp: sum(VT), v_done: sum(VT), v_pre_set: 1,
            a_ready: A_ALL, a_max: A_ALL, t_ready: 8, peak_hi: 8, peak_done: 8, peak_rows: 8 * 32,
            b_ready: B_ALL, exp_done: B_ALL, pv_done: V_ALL,
            o_copied: 8, sums_out: 8 * 64, rsum_done: 8, rsum_back: 8 * 64, bcast_done: 8, on_f: 8,
            on_hi_done: 8, on_lo_done: 8, x_bias: 1, proj_ready: 4 * NT, res_half: 4 * NT, res_done: 4 * NT,
            gu_ready: 24, gate_done: 24, hid_done: 24, h_hi_done: 24, h_lo_done: 24, out_stored: 32,
        }
        assert set(totals) == set(names.values())

        weights = [(att_a, 2 * 768, False), (att_b, 2 * 768, False), (w_dn, M_HID * 256, True),
                   (wp_a, GROUPS * 256, False), (wp_b, GROUPS * 256, False), (w_gu, 2 * 2 * HIDDEN, True)]

        block = ctx.enter_context(nc.Block())

        def end_batch(eng, go):
            eng.sem_inc(arrived, 1)
            eng.wait_ge(go, 1)
            eng.sem_clear(go)

        @block.gpsimd
        def _(pool):
            pool.memset(ident[:], 0.0).then_inc(s_pool, 1)
            pool.memset(mask_f[:], MASKED).then_inc(s_pool, 1)
            pool.wait_ge(s_pool, 1)
            pool.affine_select(out=ident[:], in_=ident[:], compare_op=ALU.not_equal, fill=1.0, base=0,
                               pattern=[[-1, P]], channel_multiplier=1).then_inc(s_pool, 1)
            pool.wait_ge(s_pool, 3)
            pool.affine_select(out=mask_f[:, 0, 0:P], in_=mask_f[:, 0, 0:P], compare_op=ALU.is_gt, fill=0.0,
                               base=0, pattern=[[1, P]], channel_multiplier=-1).then_inc(s_pool, 1)
            pool.affine_select(out=mask_f[:, 1, 0:P], in_=mask_f[:, 1, 0:P], compare_op=ALU.is_gt, fill=0.0,
                               base=0, pattern=[[-1, P]], channel_multiplier=1).then_inc(s_pool, 1)
            for n, lo in ((2, 1), (3, 0)):
                m = mask_f[:, n, :]
                half = m
                pool.affine_select(out=half, in_=m, compare_op=ALU.is_gt, fill=0.0, base=lo,
                                   pattern=[[-1, P + W]], channel_multiplier=1).then_inc(s_pool, 1)
            pool.wait_ge(s_pool, 7)
            for n, lo in ((2, 1), (3, 0)):
                m = mask_f[:, n, :]
                pool.affine_select(out=m, in_=m, compare_op=ALU.is_ge, fill=MASKED, base=lo + W - 1,
                                   pattern=[[-1, P + W]], channel_multiplier=1).then_inc(s_pool, 1)
            pool.memset(V[:], 1.0).then_inc(s_pool, 1)
            pool.memset(ones_b[:], 1.0).then_inc(s_pool, 1)
            pool.memset(onf[:], 0.0).then_inc(s_pool, 1)
            pool.memset(bias_v[:, 1, :], 0.0).then_inc(s_pool, 1)
            pool.wait_ge(s_dve, 1)

            with pool.Fori(0, B):
                for a in range(2):
                    if a == 1:
                        pool.wait_ge(res_done, NT)
                        for t in (xt_hi, xt_lo):
                            for c in (0, W + S):
                                pool.memset(t[:, :, c:c + W].bitcast(F32), 0.0).then_inc(pads, 1)
                    for m in range(4):
                        pool.wait_ge(part_mid, 4 * a + m + 1)
                        hi = (q_part[:, m // 2, 2, :], k_part[:, m // 2, 2, W:W + S])[m % 2]
                        mid = (q_part[:, m // 2, 1, :], k_part[:, m // 2, 1, W:W + S])[m % 2]
                        pool.tensor_tensor(hi, rest[:, m % 2, :], mid, ALU.subtract).then_inc(part_lo, 1)
                    if a == 0:
                        pool.wait_ge(xn_done, NT)
                        pool.tensor_tensor(X[:], X[:], bias_p[:, None, :].to_broadcast([P, NT, E]),
                                           ALU.add).then_inc(x_bias, 1)
                    for g in range(GROUPS):
                        pool.wait_ge(on_hi_done, 4 * a + g + 1)
                        pool.tensor_tensor(on_lo[:, g, :], onf[:], on_hi[:, g, :].bitcast(F32),
                                           ALU.subtract).then_inc(on_lo_done, 1)
                    for k in range(12):
                        n, m = divmod(k, M_HID)
                        pool.wait_ge(h_hi_done, 12 * a + k + 1)
                        c = slice(HALF * n, HALF * n + HALF)
                        pool.tensor_tensor(h_lo[:, m, c], hid[:, k % 2, :], h_hi[:, m, c].bitcast(F32),
                                           ALU.subtract).then_inc(h_lo_done, 1)
                end_batch(pool, go_on["pool"])

        @block.vector
        def _(dve):
            for n, (_, cols, ints) in enumerate(weights):
                i = n % 2
                dve.wait_ge(s_raw[i], 16 * (n // 2 + 1))
                if n >= 2 and n - 2 != 2:
                    dve.wait_ge(s_img[i], 64 * len([j for j in range(i, n, 2) if j != 2]))
                if ints:
                    dve.tensor_copy(raw[i][:, 0:cols], raw_i[i][:, 0:cols]).then_inc(s_split, 1)
                else:
                    dve.tensor_copy(raw[i][:, 0:1], raw[i][:, 0:1]).then_inc(s_split, 1)
                dve.wait_ge(s_split, 3 * n + 1)
                if n == 2:
                    src = raw[i][:, 0:cols].rearrange("p (m c) -> p m c", m=M_HID)
                    hi, lo = w_dn_sb[:, :, 0:256], w_dn_sb[:, :, 256:512]
                else:
                    src, hi, lo = raw[i][:, 0:cols], st_hi[i][:, 0:cols], st_lo[i][:, 0:cols]
                dve.tensor_copy(hi, src).then_inc(s_split, 1)
                dve.wait_ge(s_split, 3 * n + 2)
                dve.tensor_tensor(lo, src, hi.bitcast(F32), ALU.subtract).then_inc(s_split, 1)
            dve.wait_ge(s_pool, 13)
            dve.wait_ge(s_small, 16 * 6)
            dve.tensor_copy(ident_b[:], ident[:]).then_inc(s_split, 1)
            dve.tensor_copy(mask_a[0][:], mask_f[:, 0, 0:P]).then_inc(s_split, 1)
            dve.tensor_copy(mask_b[0][:], mask_f[:, 1, 0:P]).then_inc(s_split, 1)
            dve.tensor_copy(mask_a[1][:], mask_f[:, 2, :]).then_inc(s_split, 1)
            dve.tensor_copy(mask_b[1][:], mask_f[:, 3, :]).then_inc(s_split, 1)
            for m in range(4):
                dve.tensor_scalar(bias_q4[:, m:m + 1], bias_qk[:, m:m + 1], (QSCALE, 1.0)[m % 2], None,
                                  ALU.mult).then_inc(s_split, 1)
            done = 3 * len(weights) + 9
            dve.tensor_copy(k_pre[:, :, 0, :], k_raw[:]).then_inc(s_split, 1)
            for n in range(2):
                dve.wait_ge(s_split, done + 1)
                src = k_raw[:] if n == 0 else k_res[:, :, 0, :]
                dve.tensor_tensor(k_res[:, :, n, :], src, k_pre[:, :, n, :], ALU.subtract).then_inc(s_split, 1)
                dve.wait_ge(s_split, done + 2)
                dve.tensor_copy(k_pre[:, :, n + 1, :], k_res[:, :, n, :]).then_inc(s_split, 1)
                done += 2
            dve.wait_ge(s_split, done + 1)
            for i in range(2):
                dve.wait_ge(s_img[i], 64 * (3, 2)[1 - i])
            dve.wait_ge(s_ones, 32)
            dve.engine_nop().then_inc(s_dve, 1)

            def layer_norm(n):
                if n == 0:
                    dve.wait_ge(x_in, 16)
                for t in range(NT):
                    if n:
                        dve.wait_ge(res_done, NT * (n - 1) + t + 1)
                    dve.bn_stats(stats[:, t, :], X[:, t, :]).then_inc(stats_done, 1)
                for t in range(NT):
                    dve.wait_ge(stats_done, NT * n + t + 1)
                    dve.bn_aggr(mv[:, t, :], stats[:, t, :]).then_inc(aggr_done, 1)
                dve.wait_ge(std_done, n + 1)
                dve.reciprocal(rstd[:], std[:]).then_inc(rstd_done, 1)
                dve.wait_ge(rstd_done, n + 1)
                for t in range(NT):
                    dve.tensor_scalar(xn[:, t, :], X[:, t, :], mv[:, t, 0:1], rstd[:, t:t + 1],
                                      ALU.subtract, ALU.mult).then_inc(xn_done, 1)
                for h in range(2):
                    dve.wait_ge(xhi_done, 2 * n + h + 1)
                    c = slice(W + HALF * h, W + HALF * h + HALF)
                    dve.tensor_tensor(xt_lo[:, :, c], ring[:, h, :, :], xt_hi[:, :, c].bitcast(F32),
                                      ALU.subtract).then_inc(xlo_done, 1)

            def residual(n, t, psum):
                dve.wait_ge(proj_ready, NT * n + t + 1)
                dve.tensor_tensor(X[:, t, :], X[:, t, :], psum[:, 0:E], ALU.add).then_inc(res_half, 1)
                dve.wait_ge(res_half, NT * n + t + 1)
                dve.tensor_tensor(X[:, t, :], X[:, t, :], psum[:, E:2 * E], ALU.add).then_inc(res_done, 1)

            def normalise(a, g, part):
                if part == 0:
                    dve.wait_ge(sums_out, 64 * (4 * a + g + 1))
                    dve.reciprocal(rsum[:], sums[:]).then_inc(rsum_done, 1)
                else:
                    dve.wait_ge(rsum_back, 64 * (4 * a + g + 1))
                    dve.stream_shuffle(onf[:], onf[:], [0] * 32).then_inc(bcast_done, 1)
                    dve.wait_ge(bcast_done, 4 * a + g + 1)
                    dve.tensor_tensor(onf[:], osb[:], onf[:], ALU.mult).then_inc(on_f, 1)

            def attention(a):
                plan = PLANS[a]
                if a == 1:
                    dve.tensor_copy(k_part[:, :, :, 0:W], k_pre[:]).then_inc(kpads, 1)
                    dve.memset(k_part[:, :, :, W + S:], 0.0).then_inc(kpads, 1)
                for m in range(4):
                    dve.wait_ge(part_hi, 4 * a + m + 1)
                    if m >= 2:
                        dve.wait_ge(part_lo, 4 * a + m - 1)
                    part = (q_part[:, m // 2, :, :], k_part[:, m // 2, :, W:W + S])[m % 2]
                    dve.tensor_tensor(rest[:, m % 2, :], t32[:], part[:, 0, :],
                                      ALU.subtract).then_inc(part_rest, 1)
                    dve.wait_ge(part_rest, 4 * a + m + 1)
                    dve.tensor_copy(part[:, 1, :], rest[:, m % 2, :]).then_inc(part_mid, 1)
                for t in range(VT[a]):
                    dve.wait_ge(v_ready, VT_BASE[a] + t + 1)
                    dve.tensor_tensor(vtmp[:, t % 2, :], bias_v[:, a, :], opsum[:, t % 2, E:2 * E],
                                      ALU.add).then_inc(v_tmp, 1)
                    dve.wait_ge(v_tmp, VT_BASE[a] + t + 1)
                    dve.tensor_tensor(V[:, t, :, 0:DH],
                                      opsum[:, t % 2, 0:E].rearrange("p (h d) -> p h d", d=DH),
                                      vtmp[:, t % 2, :].rearrange("p (h d) -> p h d", d=DH),
                                      ALU.add).then_inc(v_done, 1)
                if a == 1:
                    dve.wait_ge(v_done, VT_BASE[a] + 1)
                    dve.tensor_copy(V[0:W, 0, :, 0:DH],
                                    v_pre[:].rearrange("p (h d) -> p h d", d=DH)).then_inc(v_pre_set, 1)
                for e in plan.events:
                    kind, g, k = e
                    if kind == "A":
                        i, h = plan.a_tile(k)
                        s = plan.slot[e]
                        dve.wait_ge(a_ready, A_BASE[a] + g * plan.n_a + k + 1)
                        if a == 0:
                            w = P * (i + 1)
                            dve.tensor_reduce(peak[:, g % 2, NT * h + i:NT * h + i + 1],
                                              ring[:, s, :, :].rearrange("p a c -> p (a c)")[:, 0:w],
                                              AX.X, ALU.max).then_inc(a_max, 1)
                        else:
                            dve.tensor_reduce(
                                peak[:, g % 2, :].rearrange("p (h i) -> p h i", i=NT)[:, :, i],
                                ring[:, s, :, :].rearrange("p a (c w) -> p (a c) w", c=2)[:, :, 0:P + W],
                                AX.X, ALU.max).then_inc(a_max, 1)
                        if g >= 2 and k == plan.n_a // 4:
                            normalise(a, g - 2, 0)
                        if g >= 2 and k == plan.n_a // 2:
                            normalise(a, g - 2, 1)
                    if kind == "T":
                        n = 4 * a + g
                        dve.wait_ge(t_ready, n + 1)
                        if n:
                            dve.wait_ge(peak_rows, 32 * n)
                        src = ring[0:32, plan.slot[e], 0, 0:P]
                        dve.tensor_scalar(peak_b[:, 0, :], src, -1.0, None, ALU.mult).then_inc(peak_hi, 1)
                        dve.wait_ge(peak_hi, n + 1)
                        dve.scalar_tensor_tensor(out=peak_b[:, 1, :], in0=src, scalar=-1.0,
                                                 in1=peak_b[:, 0, :], op0=ALU.mult,
                                                 op1=ALU.subtract).then_inc(peak_done, 1)
                for g in (GROUPS - 2, GROUPS - 1):
                    normalise(a, g, 0)
                    normalise(a, g, 1)
                if a == 0:
                    dve.wait_ge(x_bias, 1)
                for t in range(NT):
                    residual(2 * a, t, ring[:, t % RING, 0, :])

            def ffn(a):
                for k in range(12):
                    dve.wait_ge(gate_done, 12 * a + k + 1)
                    if k >= 2:
                        dve.wait_ge(h_lo_done, 12 * a + k - 1)
                    dve.scalar_tensor_tensor(out=hid[:, k % 2, :], in0=ring[:, (k + 2) % RING, 1, :],
                                             scalar=DEQUANT * DEQUANT, in1=gate[:, k % 2, :],
                                             op0=ALU.mult, op1=ALU.mult).then_inc(hid_done, 1)
                    if k >= 8:
                        residual(2 * a + 1, k - 8, opsum[:, k % 2, :])
                for t in range(4, NT):
                    residual(2 * a + 1, t, opsum[:, t % 2, :])

            with dve.Fori(0, B):
                for a in range(2):
                    layer_norm(2 * a)
                    attention(a)
                    layer_norm(2 * a + 1)
                    ffn(a)
                end_batch(dve, go_on["dve"])

        @block.scalar
        def _(act):
            act.wait_ge(s_dve, 1)

            def layer_norm(n):
                act.wait_ge(aggr_done, NT * (n + 1))
                act.activation(std[:], mv[:, :, 1], ACT.Sqrt, bias=EPS).then_inc(std_done, 1)
                for h in range(2):
                    act.wait_ge(turned, 2 * n + h + 1)
                    act.activation(xt_hi[:, :, W + HALF * h:W + HALF * h + HALF], ring[:, h, :, :],
                                   ACT.Copy).then_inc(xhi_done, 1)

            def attention(a):
                plan = PLANS[a]
                for m in range(4):
                    act.wait_ge(qk_ready, 4 * a + m + 1)
                    if m:
                        act.wait_ge(part_rest, 4 * a + m)
                        act.wait_ge(part_hi, 4 * a + m)
                    bias = bias_q4[:, m:m + 1] if a == 0 else 0.0
                    act.activation(t32[:], ring[:, (m + 2) % RING, :, :].rearrange("p a c -> p (a c)"),
                                   ACT.Identity, bias=bias, scale=(QSCALE, 1.0)[m % 2]).then_inc(qk_evac, 1)
                    act.wait_ge(qk_evac, 4 * a + m + 1)
                    part = (q_part[:, m // 2, 0, :], k_part[:, m // 2, 0, W:W + S])[m % 2]
                    act.activation(part, t32[:], ACT.Copy).then_inc(part_hi, 1)

                def copy_out(g):
                    act.wait_ge(pv_done, V_BASE[a] + plan.n_j * (g + 1))
                    if 4 * a + g:
                        act.wait_ge(on_f, 4 * a + g)
                    act.activation(osb[:], opsum[:].rearrange("p a c -> p (a c)"),
                                   ACT.Copy).then_inc(o_copied, 1)

                def first_part(g):
                    act.wait_ge(on_f, 4 * a + g + 1)
                    act.activation(on_hi[:, g, :], onf[:], ACT.Copy).then_inc(on_hi_done, 1)

                for e in plan.events:
                    kind, g, p = e
                    if kind != "B":
                        continue
                    j = g * plan.n_j + p // plan.per_j
                    if p == 0 and g == 0:
                        act.wait_ge(stack_in[0], 192 * (a + 1))
                        act.wait_ge(stack_in[1], 192 * (a + 1))
                    act.wait_ge(b_ready, B_BASE[a] + g * plan.n_b + p + 1)
                    if j >= 2:
                        act.wait_ge(pv_done, V_BASE[a] + j - 1)
                    jt, h = plan.b_tile(p)
                    q0, q1 = plan.queries(jt)
                    s = plan.slot[e]
                    if a == 0:
                        act.activation(probs[:, j % 2, h, 0:q1 - q0],
                                       ring[:, s, :, :].rearrange("p a c -> p (a c)")[:, 0:q1 - q0],
                                       ACT.Exp).then_inc(exp_done, 1)
                    else:
                        act.activation(probs[:, j % 2, :, 0:q1 - q0],
                                       ring[:, s, :, :].rearrange("p a (c w) -> p (a c) w", c=2)[:, :, 0:q1 - q0],
                                       ACT.Exp).then_inc(exp_done, 1)
                    if g >= 1 and p == plan.per_j - 1:
                        copy_out(g - 1)
                    if g >= 1 and p == 5 * plan.n_b // 8:
                        first_part(g - 1)
                copy_out(GROUPS - 1)
                first_part(GROUPS - 1)

            def ffn(a):
                def first_part(k):
                    n, m = divmod(k, M_HID)
                    act.wait_ge(hid_done, 12 * a + k + 1)
                    act.activation(h_hi[:, m, HALF * n:HALF * n + HALF], hid[:, k % 2, :],
                                   ACT.Copy).then_inc(h_hi_done, 1)

                for k in range(12):
                    act.wait_ge(gu_ready, 12 * a + k + 1)
                    if k >= 2:
                        act.wait_ge(hid_done, 12 * a + k - 1)
                    act.activation(gate[:, k % 2, :], ring[:, (k + 2) % RING, 0, :], ACT.Silu,
                                   scale=DEQUANT).then_inc(gate_done, 1)
                    if k:
                        first_part(k - 1)
                first_part(11)

            with act.Fori(0, B):
                for a in range(2):
                    layer_norm(2 * a)
                    attention(a)
                    layer_norm(2 * a + 1)
                    ffn(a)
                end_batch(act, go_on["act"])

        @block.tensor
        def _(pe):
            pe.wait_ge(s_dve, 1)

            def layer_norm(n):
                for h in range(2):
                    for tt in range(4):
                        t = 4 * h + tt
                        pe.wait_ge(xn_done, NT * n + t + 1)
                        for k in range(2):
                            last = pe.transpose(ring[:, h, k, P * tt:P * tt + P], xn[:, t, P * k:P * k + P],
                                                ident[:])
                    last.then_inc(turned, 1)

            def attention(a):
                plan = PLANS[a]
                pe.wait_ge(qkv_in, 16 * (a + 1))
                for m in range(4):
                    if m == 3:
                        pe.wait_ge(qk_evac, 4 * a + 1)
                    for n in range(2):
                        pe.wait_ge(xlo_done, 4 * a + n + 1)
                        dst = ring[:, (m + 2) % RING, n, :]
                        c = slice(W + HALF * n, W + HALF * n + HALF)
                        for k in range(2):
                            hi = w_qkv[:, 512 * k + P * m:512 * k + P * m + P]
                            lo = w_qkv[:, 1024 + 512 * k + P * m:1024 + 512 * k + P * m + P]
                            pe.matmul(dst, hi, xt_hi[:, k, c], start=(k == 0), stop=False)
                            pe.matmul(dst, hi, xt_lo[:, k, c], start=False, stop=False)
                            last = pe.matmul(dst, lo, xt_hi[:, k, c], start=False, stop=(k == 1))
                    last.then_inc(qk_ready, 1)
                if a == 1:
                    pe.wait_ge(pads, 4)
                for t in range(VT[a]):
                    c = P * t + (W if a == 0 else 0)
                    if t >= 2:
                        pe.wait_ge(v_done, VT_BASE[a] + t - 1)
                    dst = opsum[:, t % 2, :]
                    for k in range(2):
                        wv = w_qkv[:, 2048 + 512 * k:2048 + 512 * k + 512]
                        pe.matmul(dst, xt_hi[:, k, c:c + P], wv, start=(k == 0), stop=False)
                        last = pe.matmul(dst[:, 0:E], xt_lo[:, k, c:c + P], wv[:, 0:E], start=False,
                                         stop=(k == 1))
                    last.then_inc(v_ready, 1)

                pe.wait_ge(qk_evac, 4 * (a + 1))
                released = {"A": (a_max, A_BASE[a], plan.n_a), "B": (exp_done, B_BASE[a], plan.n_b),
                            "T": (peak_done, 4 * a, 1)}

                def slot_free(e):
                    if plan.before[e]:
                        kind, g, k = plan.before[e]
                        s, base, per = released[kind]
                        pe.wait_ge(s, base + g * per + k + 1)

                for e in plan.events:
                    kind, g, k = e
                    if kind == "A":
                        if k == 0 and g % 2 == 0:
                            pe.wait_ge(stack_in[g // 2], 192 * (a + 1))
                        slot_free(e)
                        i, h = plan.a_tile(k)
                        flat = ring[:, plan.slot[e], :, :].rearrange("p a c -> p (a c)")
                        if a == 0:
                            q = q_st[0:SP_ROWS, HG * g + h, P * i:P * i + P]
                            w = P * (i + 1)
                            for c in range(0, w, 512):
                                d = min(512, w - c)
                                pe.matmul(flat[:, c:c + d], q, k_st[0:SP_ROWS, HG * g + h, W + c:W + c + d],
                                          start=True, stop=(c + d < w), skip_group_check=True)
                            last = pe.matmul(flat[:, w - P:w], ident_b[:], mask_a[0][:], start=False, stop=True,
                                             skip_group_check=True)
                        else:
                            for h in range(HG):
                                q = q_st[0:SP_ROWS, HG * g + h, P * i:P * i + P]
                                dst = flat[:, 256 * h:256 * h + P + W]
                                pe.matmul(dst, q, k_st[0:SP_ROWS, HG * g + h, P * i:P * i + P + W],
                                          start=True, stop=False, skip_group_check=True)
                                last = pe.matmul(dst, ident_b[:], mask_a[1][:], start=False, stop=True,
                                                 skip_group_check=True)
                        last.then_inc(a_ready, 1)
                    elif kind == "T":
                        slot_free(e)
                        pe.wait_ge(a_max, A_BASE[a] + plan.n_a * (g + 1))
                        pe.transpose(ring[0:32, plan.slot[e], 0, 0:P], peak[:, g % 2, :],
                                     ident[:]).then_inc(t_ready, 1)
                    elif kind == "B":
                        if k == 0:
                            pe.wait_ge(peak_rows, 32 * (4 * a + g + 1))
                            if g == 0:
                                pe.wait_ge(ones_in, 16 * (a + 1))
                        slot_free(e)
                        j, h = plan.b_tile(k)
                        q0, q1 = plan.queries(j)
                        flat = ring[:, plan.slot[e], :, :].rearrange("p a c -> p (a c)")
                        if a == 0:
                            kk = k_st[:, HG * g + h, W + P * j:W + P * j + P]
                            w = q1 - q0
                            for c in range(0, w, 512):
                                d = min(512, w - c)
                                last = pe.matmul(flat[:, c:c + d], kk, q_st[:, HG * g + h, q0 + c:q0 + c + d],
                                                 start=True, stop=(c > 0), skip_group_check=True)
                                if c == 0:
                                    last = pe.matmul(flat[:, 0:P], ident_b[:], mask_b[0][:], start=False,
                                                     stop=True, skip_group_check=True)
                        else:
                            first = q0 - (P * j - W)
                            for h in range(HG):
                                kk = k_st[:, HG * g + h, P * j:P * j + P]
                                dst = flat[:, 256 * h:256 * h + q1 - q0]
                                pe.matmul(dst, kk, q_st[:, HG * g + h, q0:q1], start=True, stop=False,
                                          skip_group_check=True)
                                last = pe.matmul(dst, ident_b[:], mask_b[1][:, first:first + q1 - q0],
                                                 start=False, stop=True, skip_group_check=True)
                        last.then_inc(b_ready, 1)
                    else:
                        jj = g * plan.n_j + k
                        pe.wait_ge(exp_done, B_BASE[a] + plan.per_j * (jj + 1))
                        if k == 0 and g == 0:
                            pe.wait_ge(v_done, VT_BASE[a] + VT[a])
                            if a == 1:
                                pe.wait_ge(v_pre_set, 1)
                        if k == 0 and g > 0:
                            pe.wait_ge(o_copied, 4 * a + g)
                        j = NT - 1 - k if a == 0 else k
                        q0, q1 = plan.queries(j)
                        for bank in range(2):
                            c0, c1 = max(q0, 512 * bank), min(q1, 512 * bank + 512)
                            if c0 >= c1:
                                continue
                            if a == 0:
                                opens, closes = c1 == 512 * (bank + 1) and j == 4 * bank + 3, j == 0
                            else:
                                opens, closes = j == 4 * bank, j == 4 * bank + 4
                            for h in range(HG):
                                last = pe.matmul(opsum[32 * h:32 * h + 32, bank, c0 - 512 * bank:c1 - 512 * bank],
                                                 V[:, j, HG * g + h, :],
                                                 probs[:, jj % 2, h, c0 - q0:c1 - q0],
                                                 start=opens, stop=closes, skip_group_check=True)
                        last.then_inc(pv_done, 1)

                pe.wait_ge(wp_in, 16 * (a + 1))
                pe.wait_ge(on_lo_done, 4 * (a + 1))
                for t in range(NT):
                    if t >= RING:
                        pe.wait_ge(res_done, 2 * NT * a + t - 2)
                    dst = ring[:, t % RING, 0, :]
                    for g in range(GROUPS):
                        pe.matmul(dst, on_hi[:, g, P * t:P * t + P], wp_sb[:, g, :], start=(g == 0), stop=False)
                        last = pe.matmul(dst[:, 0:E], on_lo[:, g, P * t:P * t + P], wp_sb[:, g, 0:E],
                                         start=False, stop=(g == GROUPS - 1))
                    last.then_inc(proj_ready, 1)

            def ffn(a):
                def down(t):
                    pe.wait_ge(h_lo_done, 12 * a + M_HID * (t // 4 + 1))
                    if t >= 2:
                        pe.wait_ge(res_done, NT * (2 * a + 1) + t - 1)
                    dst = opsum[:, t % 2, :]
                    for m in range(M_HID):
                        pe.matmul(dst, h_hi[:, m, P * t:P * t + P], w_dn_sb[:, m, :], start=(m == 0), stop=False)
                        last = pe.matmul(dst[:, 0:E], h_lo[:, m, P * t:P * t + P], w_dn_sb[:, m, 0:E],
                                         start=False, stop=(m == M_HID - 1))
                    last.then_inc(proj_ready, 1)

                pe.wait_ge(gu_in, 16 * (a + 1))
                for k in range(12):
                    n, m = divmod(k, M_HID)
                    pe.wait_ge(xlo_done, 4 * a + 2 + (1 if k < 2 else 2))
                    if k >= RING:
                        pe.wait_ge(hid_done, 12 * a + k - 2)
                    c = slice(W + HALF * n, W + HALF * n + HALF)
                    for u in range(2):
                        dst = ring[:, (k + 2) % RING, u, :]
                        f = HIDDEN * u + P * m
                        for kk in range(2):
                            hi, lo = w_gu_sb[:, 0, kk, f:f + P], w_gu_sb[:, 1, kk, f:f + P]
                            pe.matmul(dst, hi, xt_hi[:, kk, c], start=(kk == 0), stop=False)
                            pe.matmul(dst, hi, xt_lo[:, kk, c], start=False, stop=False)
                            last = pe.matmul(dst, lo, xt_hi[:, kk, c], start=False, stop=(kk == 1))
                    last.then_inc(gu_ready, 1)
                    if k >= 8:
                        down(k - 8)
                for t in range(4, NT):
                    down(t)

            with pe.Fori(0, B):
                for a in range(2):
                    layer_norm(2 * a)
                    attention(a)
                    layer_norm(2 * a + 1)
                    ffn(a)
                end_batch(pe, go_on["pe"])

        @block.sync
        def _(sp):
            for dst, src in ((bias_qk[:], b_qk), (bias_v[:, 0, :], b_v.partition_broadcast(P)),
                             (bias_p[:], b_p.partition_broadcast(P)), (v_pre[:], v_init),
                             (k_raw[:, 0, :], k_init[0:P, :]), (k_raw[:, 1, :], k_init[P:2 * P, :])):
                sp.dma_start(dst, src).then_inc(s_small, 16)

            def store(n):
                i = n % 2
                sp.wait_ge(s_split, 3 * n + 3)
                hi, lo = st_hi[i][:].bitcast(F32), st_lo[i][:].bitcast(F32)
                if n < 2:
                    qk = img_qkv[n][:, 0:2048].rearrange("p (s k c) -> p s k c", s=2, k=2)
                    v = img_qkv[n][:, 2048:3072].rearrange("p (k s c) -> p s k c", s=2, k=2)
                    for s, t in enumerate((hi, lo)):
                        src = t[:, 0:1536].rearrange("p (k c) -> p k c", k=2)
                        sp.dma_start(qk[:, s], src[:, :, 0:512]).then_inc(s_img[i], 16)
                        sp.dma_start(v[:, s], src[:, :, 512:768]).then_inc(s_img[i], 16)
                elif n in (3, 4):
                    dst = img_wp[n - 3].rearrange("p (g s c) -> p s g c", g=GROUPS, s=2)
                    for s, t in enumerate((hi, lo)):
                        src = t[:, 0:1024].rearrange("p (g c) -> p g c", g=GROUPS)
                        sp.dma_start(dst[:, s, 0:2], src[:, 0:2]).then_inc(s_img[i], 16)
                        sp.dma_start(dst[:, s, 2:4], src[:, 2:4]).then_inc(s_img[i], 16)
                elif n == 5:
                    for s, t in enumerate((hi, lo)):
                        for k in range(2):
                            c = slice(1536 * k, 1536 * k + 1536)
                            sp.dma_start(img_gu[:, 3072 * s + 1536 * k:3072 * s + 1536 * k + 1536],
                                         t[:, c]).then_inc(s_img[i], 16)

            for n, (src, cols, ints) in enumerate(weights):
                i = n % 2
                if n >= 2:
                    sp.wait_ge(s_split, 3 * (n - 2) + 3)
                sp.dma_start((raw_i if ints else raw)[i][:, 0:cols], src).then_inc(s_raw[i], 16)
                if n >= 1:
                    store(n - 1)
            store(len(weights) - 1)
            sp.wait_ge(s_pool, 13)
            for r in range(2):
                sp.dma_start(ones_dram[r:r + 1, :].rearrange("o (a c) -> (o a) c", c=288),
                             ones_b[0:64, :, :].rearrange("p a c -> p (a c)")).then_inc(s_ones, 8 * 2)
            sp.wait_ge(s_ones, 32)
            sp.wait_ge(s_dve, 1)

            x_rows = x.rearrange("b (t p) e -> b p t e", p=P)
            out_rows = out.rearrange("b (t p) e -> b p t e", p=P)
            with sp.Fori(0, B) as b:
                sp.dma_start(X[:], x_rows[b]).then_inc(x_in, 16)
                sp.dma_start(w_qkv[:].bitcast(F32), img_qkv[0]).then_inc(qkv_in, 16)
                for a in range(2):
                    plan = PLANS[a]
                    if a == 1:
                        sp.wait_ge(res_done, 2 * NT)
                    sp.dma_start(k_st[SP_ROWS:MAX_ROWS, :, :].rearrange("p h c -> p (h c)"),
                                 ones_dram).then_inc(ones_in, 16)
                    if a == 1:
                        sp.wait_ge(kpads, 2)
                    for m in range(4):
                        heads = slice(8 * (m // 2), 8 * (m // 2) + 8)
                        sp.wait_ge(part_lo, 4 * a + m + 1)
                        for blk in range(6):
                            rows = slice(DH * blk, DH * blk + DH)
                            if m % 2 == 0:
                                dst, src = q_st[rows, heads, :], q_part[:, m // 2, Q_PART[blk], :]
                            else:
                                c = slice(W, W + S) if a == 0 else slice(0, KPAD)
                                dst, src = k_st[rows, heads, c], k_part[:, m // 2, K_PART[blk], c]
                            sp.dma_start(dst, src).then_inc(stack_in[m // 2], 16)
                    if a == 0:
                        sp.wait_ge(v_done, NT)
                        sp.dma_start(w_qkv[:].bitcast(F32), img_qkv[1]).then_inc(qkv_in, 16)

                    def peak_out(g):
                        n = 4 * a + g
                        sp.wait_ge(peak_done, n + 1)
                        for r in range(2):
                            sp.dma_start(q_st[SP_ROWS + r:SP_ROWS + r + 1, HG * g:HG * g + HG, :],
                                         peak_b[:, r, :]).then_inc(peak_rows, 16)

                    def sums_round(g):
                        n = 4 * a + g
                        sp.wait_ge(o_copied, n + 1)
                        for h in range(HG):
                            sp.dma_start(sums[32 * h:32 * h + 32, :],
                                         osb[32 * h + DH:32 * h + DH + 1, :]).then_inc(sums_out, 16)
                        sp.wait_ge(rsum_done, n + 1)
                        if n:
                            sp.wait_ge(on_lo_done, n)
                        for h in range(HG):
                            sp.dma_start(onf[32 * h:32 * h + 1, :],
                                         rsum[32 * h:32 * h + 32, :]).then_inc(rsum_back, 16)

                    peak_out(0)
                    peak_out(1)
                    for g in range(GROUPS):
                        if g == GROUPS - 1:
                            sp.wait_ge(pv_done, V_BASE[a] + GROUPS * plan.n_j)
                            sp.dma_start(wp_sb[:].rearrange("p g c -> p (g c)").bitcast(F32), img_wp[a]).then_inc(wp_in, 16)
                        sums_round(g)
                        if g + 2 < GROUPS:
                            peak_out(g + 2)
                    sp.wait_ge(exp_done, B_BASE[a] + GROUPS * plan.n_b)
                    sp.dma_start(w_gu_sb[:].rearrange("p s k c -> p (s k c)").bitcast(F32), img_gu).then_inc(gu_in, 16)
                for h in range(2):
                    sp.wait_ge(res_done, 3 * NT + 4 * (h + 1))
                    sp.dma_start(out_rows[b, :, 4 * h:4 * h + 4], X[:, 4 * h:4 * h + 4, :]).then_inc(out_stored, 16)
                sp.wait_ge(arrived, 4)
                for s, n in totals.items():
                    sp.wait_ge(s, n)
                for s in totals:
                    sp.sem_clear(s)
                sp.sem_clear(arrived)
                for go in go_on.values():
                    sp.sem_inc(go, 1)


def kernel(L0_attn_a_x, L0_attn_a_W1, L0_attn_a_b1, L0_attn_a_Wp, L0_attn_a_bp, L0_attn_b_Wq, L0_attn_b_Wk,
           L0_attn_b_Wv, L0_attn_b_Wo, L0_attn_b_last_k_init, L0_attn_b_last_v_init, L0_ffn_w_gate, L0_ffn_w_up,
           L0_ffn_w_down):
    import concourse.bacc as bacc
    from concourse.bass_utils import run_bass_kernel_spmd

    def halves(w):
        w = np.asarray(w).reshape(-1, 2, 8, DH).transpose(0, 1, 3, 2)
        return w.reshape(w.shape[0], 2, P)

    def rows(w):
        w = np.asarray(w)
        return np.ascontiguousarray(w.reshape(-1, P, w.shape[1]).transpose(1, 0, 2).reshape(P, -1))

    def qkv(q, k, v):
        q, k = halves(q), halves(k)
        qk = np.stack([q, k], axis=2).reshape(q.shape[0], 4 * P)
        return rows(np.concatenate([qk, np.asarray(v)], axis=1))

    def padded(w):
        w = np.asarray(w).reshape(GROUPS, HG, DH, E)
        return rows(np.concatenate([w, np.zeros_like(w)], axis=2).reshape(GROUPS * P, E))

    w1 = np.asarray(L0_attn_a_W1).reshape(E, HEADS, 3, DH)
    b1 = np.asarray(L0_attn_a_b1).reshape(1, HEADS, 3, DH)
    q1, k1, v1 = (w1[:, :, i].reshape(E, E) for i in range(3))
    bq, bk, bv = (b1[:, :, i].reshape(1, E) for i in range(3))
    b_qk = np.ascontiguousarray(np.stack([halves(bq)[0], halves(bk)[0]], axis=1).reshape(4, P).T)
    last_k = np.asarray(L0_attn_b_last_k_init)
    last_v = np.asarray(L0_attn_b_last_v_init).reshape(W - 1, E)
    kt = halves(last_k.reshape(W - 1, E)).reshape(W - 1, E).T
    data = {
        "x": np.asarray(L0_attn_a_x),
        "att_a": qkv(q1, k1, v1),
        "att_b": qkv(np.asarray(L0_attn_b_Wq).T, np.asarray(L0_attn_b_Wk).T, np.asarray(L0_attn_b_Wv).T),
        "b_qk": b_qk,
        "b_v": np.ascontiguousarray(bv).reshape(E),
        "wp_a": padded(L0_attn_a_Wp),
        "wp_b": padded(np.asarray(L0_attn_b_Wo).T),
        "b_p": np.asarray(L0_attn_a_bp),
        "w_gu": rows(np.concatenate([np.asarray(L0_ffn_w_gate).T, np.asarray(L0_ffn_w_up).T], axis=1)),
        "w_dn": rows(np.asarray(L0_ffn_w_down).T),
        "k_init": np.ascontiguousarray(np.concatenate([np.zeros_like(kt[:, :1]), kt], axis=1)),
        "v_init": np.concatenate([np.zeros_like(last_v[:1]), last_v], axis=0),
    }
    nc = bacc.Bacc("TRN2", target_bir_lowering=False, num_devices=1)
    arrays, args = {}, []
    for name, a in data.items():
        a = np.ascontiguousarray(a)
        arrays[f"in_{name}"] = a
        args.append(nc.dram_tensor(f"in_{name}", a.shape, mybir.dt.from_np(a.dtype), kind="ExternalInput").ap())
    args.append(nc.dram_tensor("y", (B, S, E), F32, kind="ExternalOutput").ap())
    layers_kernel(nc, *args)
    got = run_bass_kernel_spmd(nc, [arrays], core_ids=[0])
    return got.results[0]["y"]
```

```python
from contextlib import ExitStack

import numpy as np

import concourse.bass as bass
from concourse import mybir

P = 128
B, S, E = 4, 1024, 256
HEADS, DH = 16, 16
GROUPS, HG = 4, 4
W = 64
HIDDEN = 768
NT = S // P
HALF = S // 2
KPAD = W + S + W
SP_ROWS = 6 * DH
MAX_ROWS = SP_ROWS + 2
Q_PART = (0, 1, 0, 1, 2, 0)
K_PART = (0, 0, 1, 1, 0, 2)
M_HID = HIDDEN // P
EPS = 1e-5
QSCALE = 0.25
DEQUANT = float(np.float32(1.0 / 127.0))
MASKED = -1.0e30
RING = 3
V_FIRST = 4

ALU = mybir.AluOpType
ACT = mybir.ActivationFunctionType
AX = mybir.AxisListType
F32 = mybir.dt.float32
F32R = mybir.dt.float32r
BF16 = mybir.dt.bfloat16
I32 = mybir.dt.int32


class Plan:

    def __init__(self, causal):
        self.causal = causal
        self.vt = NT if causal else NT + 1
        self.n_j = NT if causal else NT + 1
        self.last = (3, 7) if causal else (4, 8)
        self.opens = (0, 0) if causal else (0, 4)
        self.a_units = [u for i in range(NT) for u in self.units(i, P * (i + 1) if causal else P + W)]
        self.b_units = [u for j in range(self.n_j) for u in self.units(j, self.b_width(j))]
        self.n_a, self.n_b = len(self.a_units), len(self.b_units)
        self.b_upto = [1 + max(n for n, u in enumerate(self.b_units) if u[0] == j) for j in range(self.n_j)]
        ahead = [0.9 + 0.05 * n for n in range(20)]
        _, self.events = min((self.order(lead) for lead in ahead), key=lambda x: x[0])
        self.ring = [e for e in self.events if e[0] in "QATB"]
        kinds = ["MD" if e[0] in "MD" else e[0] for e in self.events]
        self.nth = {e: kinds[:n].count(kinds[n]) for n, e in enumerate(self.events)}
        self.slot = {e: (n + 2) % RING for n, e in enumerate(self.ring)}
        self.before = {e: self.ring[n - RING] if n >= RING else None for n, e in enumerate(self.ring)}

    def units(self, tile, width):
        per = 4 if width <= 256 else 2 if width <= 512 else 1
        return [(tile, h, per, 1024 // per) for h in range(0, HG, per)]

    def a_width(self, i):
        return P * (i + 1) if self.causal else P + W

    def queries(self, j):
        if self.causal:
            return P * j, S
        return max(0, P * j - W), min(S, P * j + P)

    def b_width(self, j):
        return self.queries(j)[1] - self.queries(j)[0]

    def order(self, lead):
        events = []
        pe = dve = act = 0.0
        free = [0.0] * RING
        later = []
        rows_at = {}
        stacked = {}
        a_next, b_next = 0, 0
        a_work, b_work = 0.0, 0.0
        a_all = sum(u[2] * self.a_width(u[0]) for u in self.a_units)
        b_all = sum(u[2] * self.b_width(u[0]) for u in self.b_units)

        def early(kind, p, n):
            nonlocal pe, dve, act
            events.append((kind, p, n))
            if kind == "Q":
                pe = max(pe, free[-RING]) + 2.7
                act = max(act, pe) + 1.8
                dve = max(dve, act - 0.9) + 1.8
                free.append(act)
                stacked[p, n] = max(dve + 2.0, max(stacked.values(), default=0.0) - 2.0) + 8.5
            else:
                pe += 0.9
                act = max(act, pe) + 0.3
                dve = max(dve, act) + 0.35

        def flush(now, force=lambda e: False):
            nonlocal pe, dve, act
            while later:
                later.sort(key=lambda x: x[0])
                n = next((n for n, (at, e) in enumerate(later) if at <= now or force(e)), None)
                if n is None:
                    return
                at, e = later.pop(n)
                kind, g, k = e
                events.append(e)
                if kind == "T":
                    pe = max(pe, at, free[-RING]) + 0.3
                    dve = max(dve, pe) + 0.5
                    free.append(dve)
                    rows_at[g] = dve + 2.8
                elif kind == "V":
                    pe = max(pe, at) + 0.0017 * self.b_width(k)
                    if k in self.last:
                        later.append((pe + 0.2, ("C" if g < GROUPS - 1 else "D", g, self.last.index(k))))
                elif kind == "C":
                    act = max(act, at) + 0.5
                    later.append((act + 2.8, ("R", g, k)))
                elif kind == "R":
                    dve = max(dve, at) + 0.15
                    later.append((dve + 2.8, ("M", g, k)))
                elif kind == "M":
                    dve = max(dve, at) + 1.2
                    later.append((dve + 0.1, ("H", g, k)))
                elif kind == "D":
                    dve = max(dve, at) + 4.6
                    later.append((dve + 0.1, ("H", g, k)))
                elif kind == "H":
                    act = max(act, at) + 0.5
                    later.append((act + 1.5, ("K", g, k)))
                elif kind == "K" and (g, k) == (GROUPS - 1, 0):
                    for t in range(4):
                        later.append((at + 3.0 + 0.9 * t, ("O", 0, t)))
                elif kind == "O":
                    pe = max(pe, at) + 0.9
                    dve = max(dve, pe) + 1.1

        after = 2 if self.causal else 0
        early("Q", 0, 0)
        for t in range(V_FIRST - after):
            early("P", 0, t)
        early("Q", 0, 1)
        for t in range(V_FIRST - after, V_FIRST):
            early("P", 0, t)
        fill = [("P", 0, t) for t in range(V_FIRST, self.vt)]
        fill = [("Q", 1, 0)] + fill[:2] + [("Q", 1, 1)] + fill[2:]

        while a_next < GROUPS * self.n_a or b_next < GROUPS * self.n_b:
            ga, ka = divmod(a_next, self.n_a)
            gb, kb = divmod(b_next, self.n_b)
            start = max(pe, free[-RING])
            a_at = float("inf")
            if ga < GROUPS and (ga < 2 or (ga - 2) in rows_at):
                need = (ga // 2, 1 if self.a_units[ka][0] >= 4 else 0)
                a_at = max(start, stacked.get(need, float("inf")))
            can_b = gb < GROUPS and gb in rows_at and rows_at[gb] <= max(start, act)
            if fill and not can_b and a_at > pe + 0.3:
                early(*fill.pop(0))
                continue
            flush(start)
            can_a = a_at <= start + 0.3 or (a_at < float("inf") and not can_b)
            if not can_a and not can_b:
                if gb not in rows_at:
                    flush(start, lambda e: e[0] == "T" and e[1] == gb)
                can_b = True
            if can_a and (not can_b or a_work < b_work + lead):
                i, _, heads, _ = self.a_units[ka]
                w = heads * self.a_width(i)
                pe = max(pe, free[-RING], a_at) + 0.05 + 0.12 * heads + 0.00042 * w
                dve = max(dve, pe + 0.1) + 0.1 + 0.00104 * w
                free.append(dve)
                events.append(("A", ga, ka))
                a_next += 1
                a_work += w / a_all
                if ka == self.n_a - 1:
                    later.append((dve + 0.1, ("T", ga, 0)))
            else:
                while b_next == 0 and fill:
                    early(*fill.pop(0))
                j, _, heads, _ = self.b_units[kb]
                if kb == 0 or self.b_units[kb - 1][0] != j:
                    flush(start, lambda e: e[0] == "V" and (e[1] < gb and (e[2] < self.n_j - 1 or j > 0)
                                                             or e[1] == gb and e[2] < j - 1))
                w = heads * self.b_width(j)
                pe = max(pe, free[-RING], rows_at[gb]) + 0.05 + 0.08 * heads + 0.00042 * w
                act = max(act, pe + 0.1) + 0.2 + 0.00071 * w
                free.append(act)
                events.append(("B", gb, kb))
                b_next += 1
                b_work += w / b_all
                if kb + 1 in self.b_upto:
                    later.append((act + (1.2 if self.causal else 0.1), ("V", gb, j)))
        flush(float("inf"))
        return max(pe, dve, act), events


PLANS = (Plan(True), Plan(False))
A_BASE = (0, GROUPS * PLANS[0].n_a)
B_BASE = (0, GROUPS * PLANS[0].n_b)
V_BASE = (0, GROUPS * PLANS[0].n_j)
A_ALL = A_BASE[1] + GROUPS * PLANS[1].n_a
B_ALL = B_BASE[1] + GROUPS * PLANS[1].n_b
V_ALL = V_BASE[1] + GROUPS * PLANS[1].n_j
VT = (NT, NT + 1)
VT_BASE = (0, NT)
COPIED, NORMED = 2 * GROUPS - 2, 2 * GROUPS


GU_SLOT = (0, 2, 0, 2, 1, 0, 2, 1, 0, 2, 1, 0)


def layers_kernel(nc, x, att_a, att_b, b_qk, b_v, wp_a, wp_b, b_p, w_gu, w_dn, k_init, v_init, out):
    img_qkv = [nc.dram_tensor(f"img_qkv{a}", [P, 3072], F32, kind="Internal").ap() for a in range(2)]
    img_wp = [nc.dram_tensor(f"img_wp{a}", [P, 1024], F32, kind="Internal").ap() for a in range(2)]
    img_gu = nc.dram_tensor("img_gu", [P, 6144], F32, kind="Internal").ap()
    ones_dram = nc.dram_tensor("ones_dram", [2, HEADS * KPAD], BF16, kind="Internal").ap()

    with ExitStack() as ctx:
        where = [16512]

        def region(size):
            at = where[0]
            where[0] += (size + 31) // 32 * 32
            assert where[0] <= nc.sbuf_usable_end, where[0]
            return at

        def at(name, address, shape, dt):
            return nc.alloc_sbuf_tensor_at(name, shape, dt, offset=address)

        def sb(name, shape, dt):
            n = int(np.prod(shape[1:])) * (2 if dt == BF16 else 4)
            return at(name, region(n), shape, dt)

        def sem(name):
            return ctx.enter_context(nc.semaphore(name))

        ring = ctx.enter_context(nc.psum_tensor("ring", [P, RING, 2, 512], F32))
        opsum = ctx.enter_context(nc.psum_tensor("opsum", [P, 2, 512], F32))

        X = sb("X", [P, NT, E], F32)
        r_xt = region(18432 + 12288)
        xt_hi = at("xt_hi", r_xt, [P, 2, KPAD], F32R)
        xt_lo = at("xt_lo", r_xt + 2 * KPAD * 4, [P, 2, KPAD], F32R)
        t32 = at("t32", r_xt + 18432, [P, 2, HALF], F32)
        rest = at("rest", r_xt + 18432 + 4096, [P, 4, HALF], F32)
        wp_sb = at("wp_sb", r_xt + 18432, [P, 2, 512], F32R)
        o_hi = at("o_hi", r_xt + 18432 + 8192, [P, 2, HALF], F32R)
        r_z = region(73728)
        q_st = at("q_st", r_z, [MAX_ROWS, HEADS, S], BF16)
        k_st = at("k_st", r_z + HEADS * S * 2, [MAX_ROWS, HEADS, KPAD], BF16)
        w_gu_sb = at("w_gu_sb", r_z, [P, 2, 2, 2 * HIDDEN], F32R)
        h_hi = at("h_hi", r_z + 24576, [P, M_HID, S], F32R)
        h_lo = at("h_lo", r_z + 49152, [P, M_HID, S], F32R)
        st_hi = [at(f"st_hi{i}", r_z + 36864 * i + 12288, [P, 3072], F32R) for i in range(2)]
        st_lo = [at(f"st_lo{i}", r_z + 36864 * i + 24576, [P, 3072], F32R) for i in range(2)]
        r_p = region(32768)
        probs = at("probs", r_p, [P, 2, HG, S], F32)
        q_part = at("q_part", r_p, [P, 2, 3, S], BF16)
        k_part = at("k_part", r_p + 12288, [P, 2, 3, KPAD], BF16)
        gate = at("gate", r_p, [P, 2, HALF], F32)
        hid = at("hid", r_p + 4096, [P, 2, HALF], F32)
        xn = at("xn", r_p + 28672, [P, 4, E], F32)
        raw_at = (r_p + 12288, r_z, r_z + 6144, r_z + 36864, r_z + 43008, r_z + 45056)
        raw = [at(f"raw{n}", place, [P, width], F32) for n, (place, width) in
               enumerate(zip(raw_at, (3072, 1536, 1536, 1536, 512, 512)))]
        raw_i = {n: at(f"raw_i{n}", raw_at[n], raw[n].shape, I32) for n in (0, 3)}
        V = sb("V", [P, NT + 1, HEADS, DH, 2], F32)
        r_w = region(16384)
        w_qkv = at("w_qkv", r_w, [P, 3072], F32R)
        on_hi = at("on_hi", r_w, [P, 2, S], F32R)
        on_lo = at("on_lo", r_w + 8192, [P, 2, S], F32R)
        w_dn_sb = sb("w_dn_sb", [P, M_HID, 512], F32R)
        r_o = region(8192)
        osb = at("osb", r_o, [P, 2, HALF], F32)
        onf = at("onf", r_o + 4096, [P, 2, HALF], F32)
        x_next = at("x_next", r_o, [P, NT, E], F32)
        ident = sb("ident", [P, P], F32)
        ident_b = sb("ident_b", [P, P], BF16)
        mask_a = [sb("mask_a0", [P, P], BF16), sb("mask_a1", [P, P + W], BF16)]
        mask_b = sb("mask_b", [P, P + W], BF16)
        peak = sb("peak", [P, 2, 32], F32)
        peak_b = sb("peak_b", [32, 2, P], BF16)
        bias_p = sb("bias_p", [P, E], F32)
        bias_qk = sb("bias_qk", [P, 4], F32)
        bias_q4 = sb("bias_q4", [P, 4], F32)
        v_pre = sb("v_pre", [W, E], F32)
        k_pre = sb("k_pre", [P, 2, 3, W], BF16)
        stats = sb("stats", [P, NT, 6], F32)
        mv = sb("mv", [P, NT, 2], F32)
        std = sb("std", [P, NT], F32)
        rstd = sb("rstd", [P, NT], F32)
        sums = sb("sums", [P, 2, 16], F32)
        rsum = sb("rsum", [P, 2, 16], F32)
        table = sb("table", [P, 9], F32)
        second = sb("second", [P, 2], F32)
        wide = sb("wide", [1, 1], I32)
        k_raw = at("k_raw", r_p, [P, 2, W], F32)
        k_res = at("k_res", r_p + 1024, [P, 2, 2, W], F32)
        mask_f = at("mask_f", r_p + 4096, [P, 3, P + W], F32)
        ones_b = at("ones_b", r_p + 8192, [P, 2, 144], BF16)
        bv_col = at("bv_col", r_p + 9216, [P, 2], F32)
        bv_all = at("bv_all", r_p + 9344, [P, 2, P], F32)

        s_small = sem("small_loaded")
        s_raw = [sem(f"raw_loaded{n}") for n in range(6)]
        s_first = sem("weights_first_part")
        s_split = sem("weights_split")
        s_img = [sem("image_stored0"), sem("image_stored1")]
        s_pool = sem("pool_setup")
        s_bias = sem("value_bias_projected")
        s_wide = sem("second_part_of_gate_and_up")
        s_dve = sem("dve_setup")
        s_ones = sem("ones_stored")
        arrived = sem("engines_arrived")
        go_on = {n: sem(f"go_on_{n}") for n in ("pool", "dve", "act", "pe")}
        out_stored = sem("out_stored")
        x_free = sem("x_free")

        names = {}
        for n in ("x_in qkv_in wp_in gu_in ones_in kpads stats_done aggr_done std_done rstd_done xn_done "
                  "turned xhi_done xlo_done qk_ready qk_evac part_hi part_rest part_mid part_lo stack0 stack1 stack2 "
                  "v_ready v_half v_done masked direct a_ready a_max t_ready peak_hi peak_done peak_rows "
                  "b_ready exp_done pv_done o_copied sums_out0 sums_out1 rsum_done rsum_back0 rsum_back1 "
                  "bcast_done on_f on_hi_done on_lo_done packed0 packed1 x_bias proj_ready res_half res_done "
                  "gu_ready gate_done hid_done h_hi_done h_lo_done table_in").split():
            names[n] = sem(n)
        (x_in, qkv_in, wp_in, gu_in, ones_in, kpads, stats_done, aggr_done, std_done, rstd_done, xn_done,
         turned, xhi_done, xlo_done, qk_ready, qk_evac, part_hi, part_rest, part_mid, part_lo, stack0, stack1, stack2,
         v_ready, v_half, v_done, masked, direct, a_ready, a_max, t_ready, peak_hi, peak_done, peak_rows,
         b_ready, exp_done, pv_done, o_copied, sums_out0, sums_out1, rsum_done, rsum_back0, rsum_back1,
         bcast_done, on_f, on_hi_done, on_lo_done, packed0, packed1, x_bias, proj_ready, res_half, res_done,
         gu_ready, gate_done, hid_done, h_hi_done, h_lo_done, table_in) = names.values()
        stack_in = (stack0, stack1, stack2)
        sums_out = (sums_out0, sums_out1)
        rsum_back = (rsum_back0, rsum_back1)
        packed = (packed0, packed1)
        totals = {
            x_in: 16, qkv_in: 32, wp_in: 32, gu_in: 64, ones_in: 32, kpads: 2,
            stats_done: 4 * NT, aggr_done: 4 * NT, std_done: 8, rstd_done: 8, xn_done: 4 * NT,
            turned: 8, xhi_done: 8, xlo_done: 8,
            qk_ready: 16, qk_evac: 16, part_hi: 16, part_rest: 16, part_mid: 16, part_lo: 16,
            stack0: 2 * 192, stack1: 2 * 192, stack2: 2 * 192, v_ready: sum(VT), v_half: sum(VT) + 1, v_done: sum(VT),
            masked: V_BASE[1], direct: 4,
            a_ready: A_ALL, a_max: A_ALL, t_ready: 8, peak_hi: 8, peak_done: 8, peak_rows: 8 * 32,
            b_ready: B_ALL, exp_done: B_ALL, pv_done: V_ALL,
            o_copied: 12, sums_out0: 96, sums_out1: 96, rsum_done: 12, rsum_back0: 96, rsum_back1: 96,
            bcast_done: 16, on_f: 16, on_hi_done: 16, on_lo_done: 16, packed0: 256, packed1: 256, x_bias: 2,
            proj_ready: 4 * NT, res_half: 4 * NT, res_done: 4 * NT,
            gu_ready: 24, gate_done: 24, hid_done: 24, h_hi_done: 24, h_lo_done: 24, table_in: 8,
        }
        assert set(totals) == set(names.values())
        first = {x_in: 16, qkv_in: 16, stats_done: NT, aggr_done: NT, std_done: 2, rstd_done: 2, xn_done: NT,
                 turned: 2, xhi_done: 2, xlo_done: 2}
        counted = range(min(s.num for s in totals), max(s.num for s in totals) + 1)
        assert len(counted) == len(totals)

        weights = [(w_gu, 2 * 2 * HIDDEN, True), (att_a, 2 * 768, False), (att_b, 2 * 768, False),
                   (w_dn, M_HID * 256, True), (wp_a, 2 * 256, False), (wp_b, 2 * 256, False)]

        block = ctx.enter_context(nc.Block())

        def end_batch(eng, go):
            eng.sem_inc(arrived, 1)
            eng.wait_ge(go, 1)
            eng.sem_clear(go)

        def split_at(n):
            i, width = n % 2, weights[n][1]
            if n == 3:
                return (raw[n][:].rearrange("p (m c) -> p m c", m=M_HID),
                        w_dn_sb[:, :, 0:256], w_dn_sb[:, :, 256:512])
            return raw[n][:], st_hi[i][:, 0:width], st_lo[i][:, 0:width]

        def stored_before(n):
            return 64 * len([m for m in range(n % 2, n, 2) if m != 3])

        def flat(slot):
            return ring[:, slot, :, :].rearrange("p a c -> p (a c)")

        def heads_of(slot, unit, width):
            return flat(slot).rearrange("p (h c) -> p h c", c=unit[3])[:, 0:unit[2], 0:width]

        def part_of(n):
            heads, h, which = n // 4, n // 2 % 2, n % 2
            if which == 0:
                return q_part[:, heads, :, HALF * h:HALF * h + HALF]
            return k_part[:, heads, :, cols(h)]

        def proj_bank(t):
            return (ring[:, 2, 0, :], ring[:, 2, 1, :], opsum[:, 0, :])[t % 3]

        def normed(g):
            return osb if g == GROUPS - 1 else onf

        def cols(h):
            return slice(W + HALF * h, W + HALF * h + HALF)

        @block.gpsimd
        def _(pool):
            pool.memset(ident[:], 0.0).then_inc(s_pool, 1)
            pool.memset(mask_f[:], MASKED).then_inc(s_pool, 1)
            pool.wait_ge(s_pool, 1)
            pool.affine_select(out=ident[:], in_=ident[:], compare_op=ALU.not_equal, fill=1.0, base=0,
                               pattern=[[-1, P]], channel_multiplier=1).then_inc(s_pool, 1)
            pool.wait_ge(s_pool, 3)
            pool.affine_select(out=mask_f[:, 0, 0:P], in_=mask_f[:, 0, 0:P], compare_op=ALU.is_gt, fill=0.0,
                               base=0, pattern=[[1, P]], channel_multiplier=-1).then_inc(s_pool, 1)
            for n, lo in ((1, 1), (2, 0)):
                m = mask_f[:, n, :]
                pool.affine_select(out=m, in_=m, compare_op=ALU.is_gt, fill=0.0, base=lo,
                                   pattern=[[-1, P + W]], channel_multiplier=1).then_inc(s_pool, 1)
            pool.wait_ge(s_pool, 6)
            for n, lo in ((1, 1), (2, 0)):
                m = mask_f[:, n, :]
                pool.affine_select(out=m, in_=m, compare_op=ALU.is_ge, fill=MASKED, base=lo + W - 1,
                                   pattern=[[-1, P + W]], channel_multiplier=1).then_inc(s_pool, 1)
            pool.memset(ones_b[:], 1.0).then_inc(s_pool, 1)
            pool.memset(table[:], 0.0).then_inc(s_pool, 1)
            for t in (xt_hi, xt_lo):
                for c in (0, W + S):
                    pool.memset(t[:, :, c:c + W].bitcast(F32), 0.0).then_inc(s_pool, 1)
            pool.memset(V[:], 1.0).then_inc(s_pool, 1)
            pool.wait_ge(s_dve, 1)
            end_batch(pool, go_on["pool"])

            def k_pads():
                pool.wait_ge(pv_done, V_BASE[1])
                pool.tensor_copy(k_part[:, :, :, 0:W], k_pre[:]).then_inc(kpads, 1)
                pool.memset(k_part[:, :, :, W + S:], 0.0).then_inc(kpads, 1)

            with pool.Fori(0, B):
                for a in range(2):
                    for n in range(8):
                        pool.wait_ge(part_mid, 8 * a + n + 1)
                        part = part_of(n)
                        pool.tensor_tensor(part[:, 2, :], rest[:, n % 4, :], part[:, 1, :],
                                           ALU.subtract).then_inc(part_lo, 1)
                    if a == 0:
                        pool.wait_ge(x_free, 1)
                        pool.tensor_tensor(X[:], x_next[:], bias_p[:, None, :].to_broadcast([P, NT, E]),
                                           ALU.add).then_inc(x_bias, 1)
                        pool.sem_clear(x_free)
                        pool.wait_ge(x_bias, 1)
                        pool.memset(onf[:], 0.0).then_inc(x_bias, 1)
                    plan = PLANS[a]
                    for e in plan.events:
                        kind, g, k = e
                        if kind == "H":
                            pool.wait_ge(on_hi_done, NORMED * a + plan.nth[e] + 1)
                            o = normed(g)[:, k, :]
                            pool.tensor_tensor(o.bitcast(F32R), o, o_hi[:, k, :].bitcast(F32),
                                               ALU.subtract).then_inc(on_lo_done, 1)
                        elif a == 0 and kind == "B" and k + 1 in plan.b_upto:
                            j = plan.b_units[k][0]
                            pool.wait_ge(exp_done, g * plan.n_b + k + 1)
                            block = probs[:, (g * plan.n_j + j) % 2, :, 0:P]
                            pool.affine_select(out=block, in_=block, compare_op=ALU.is_ge, fill=0.0, base=0,
                                               pattern=[[0, HG], [1, P]],
                                               channel_multiplier=-1).then_inc(masked, 1)
                    if a == 0:
                        k_pads()
                    for k in range(12):
                        n, m = divmod(k, M_HID)
                        pool.wait_ge(h_hi_done, 12 * a + k + 1)
                        c = slice(HALF * n, HALF * n + HALF)
                        pool.tensor_tensor(h_lo[:, m, c], hid[:, k % 2, :], h_hi[:, m, c].bitcast(F32),
                                           ALU.subtract).then_inc(h_lo_done, 1)
                end_batch(pool, go_on["pool"])

        @block.vector
        def _(dve):
            def stats_of(n, t):
                src = x_next if n == 3 else X
                if n < 3:
                    dve.wait_ge(res_done, NT * n + t + 1)
                dve.bn_stats(stats[:, t, :], src[:, t, :]).then_inc(stats_done, 1)
                dve.wait_ge(stats_done, NT * (n % 4) + t + 1)
                dve.bn_aggr(mv[:, t, :], stats[:, t, :]).then_inc(aggr_done, 1)

            def scale(n, h, base):
                src = x_next if n == 3 else X
                dve.wait_ge(std_done, 2 * base + h + 1)
                dve.reciprocal(rstd[:, 4 * h:4 * h + 4], std[:, 4 * h:4 * h + 4]).then_inc(rstd_done, 1)
                dve.wait_ge(rstd_done, 2 * base + h + 1)
                if 2 * base + h:
                    dve.wait_ge(turned, 2 * base + h)
                for t in range(4 * h, 4 * h + 4):
                    dve.tensor_scalar(xn[:, t % 4, :], src[:, t, :], mv[:, t, 0:1], rstd[:, t:t + 1],
                                      ALU.subtract, ALU.mult).then_inc(xn_done, 1)

            def second_part(h, base):
                dve.wait_ge(xhi_done, 2 * base + h + 1)
                dve.tensor_tensor(xt_lo[:, :, cols(h)], ring[:, h, :, :], xt_hi[:, :, cols(h)].bitcast(F32),
                                  ALU.subtract).then_inc(xlo_done, 1)

            def residual(n, t, psum):
                dve.wait_ge(proj_ready, NT * n + t + 1)
                dve.tensor_tensor(X[:, t, :], X[:, t, :], psum[:, 0:E], ALU.add).then_inc(res_half, 1)
                dve.wait_ge(res_half, NT * n + t + 1)
                dve.tensor_tensor(X[:, t, :], X[:, t, :], psum[:, E:2 * E], ALU.add).then_inc(res_done, 1)

            def value(a, t):
                dve.wait_ge(v_half, VT_BASE[a] + a + t + 1)
                rows = slice(W if a == 1 and t == 0 else 0, P)
                dve.tensor_tensor(V[rows, t, :, :, 0], V[rows, t, :, :, 0],
                                  opsum[rows, t % 2, E:2 * E].rearrange("p (h d) -> p h d", d=DH),
                                  ALU.add).then_inc(v_done, 1)

            def parts(a, n):
                dve.wait_ge(part_hi, 8 * a + n + 1)
                if n >= 4:
                    dve.wait_ge(part_lo, 8 * a + n - 3)
                part = part_of(n)
                dve.tensor_tensor(rest[:, n % 4, :], t32[:, n % 2, :], part[:, 0, :],
                                  ALU.subtract).then_inc(part_rest, 1)
                dve.wait_ge(part_rest, 8 * a + n + 1)
                dve.tensor_copy(part[:, 1, :], rest[:, n % 4, :]).then_inc(part_mid, 1)

            def attention(a):
                plan = PLANS[a]
                for e in plan.events:
                    kind, g, k = e
                    if kind == "P":
                        value(a, k)
                    elif kind == "Q":
                        if a == 1 and (g, k) == (0, 1):
                            second_part(1, 1)
                        for which in range(2):
                            parts(a, 4 * g + 2 * k + which)
                    elif kind == "A":
                        i, h, heads, _ = unit = plan.a_units[k]
                        dve.wait_ge(a_ready, A_BASE[a] + g * plan.n_a + k + 1)
                        dve.tensor_reduce(peak[:, g % 2, :].rearrange("p (h i) -> p h i", i=NT)[:, h:h + heads, i],
                                          heads_of(plan.slot[e], unit, plan.a_width(i)),
                                          AX.X, ALU.max).then_inc(a_max, 1)
                    elif kind == "T":
                        n = 4 * a + g
                        dve.wait_ge(t_ready, n + 1)
                        if n:
                            dve.wait_ge(peak_rows, 32 * n)
                        src = ring[0:32, plan.slot[e], 0, 0:P]
                        dve.tensor_scalar(peak_b[:, 0, :], src, -1.0, None, ALU.mult).then_inc(peak_hi, 1)
                        dve.wait_ge(peak_hi, n + 1)
                        dve.scalar_tensor_tensor(out=peak_b[:, 1, :], in0=src, scalar=-1.0,
                                                 in1=peak_b[:, 0, :], op0=ALU.mult,
                                                 op1=ALU.subtract).then_inc(peak_done, 1)
                    elif kind == "R":
                        dve.wait_ge(sums_out[k], 16 * ((GROUPS - 1) * a + g + 1))
                        dve.reciprocal(rsum[:, k, :], sums[:, k, :]).then_inc(rsum_done, 1)
                    elif kind == "M":
                        dve.wait_ge(rsum_back[k], 16 * ((GROUPS - 1) * a + g + 1))
                        dve.stream_shuffle(onf[:, k, :], onf[:, k, :], [0] * 32).then_inc(bcast_done, 1)
                        dve.wait_ge(bcast_done, NORMED * a + plan.nth[e] + 1)
                        dve.tensor_tensor(onf[:, k, :], osb[:, k, :], onf[:, k, :], ALU.mult).then_inc(on_f, 1)
                    elif kind == "D":
                        dve.wait_ge(pv_done, V_BASE[a] + plan.n_j * g + plan.last[k] + 1)
                        dve.wait_ge(on_f, NORMED * a + plan.nth["M", g - 1, k] + 1)
                        dve.stream_shuffle(osb[:, k, :], opsum[:, k, :], [1] * 32).then_inc(bcast_done, 1)
                        dve.wait_ge(bcast_done, NORMED * a + plan.nth[e] + 1)
                        dve.reciprocal(osb[:, k, :], osb[:, k, :]).then_inc(direct, 1)
                        dve.wait_ge(direct, 2 * a + k + 1)
                        dve.tensor_tensor(osb[:, k, :], opsum[:, k, :], osb[:, k, :], ALU.mult).then_inc(on_f, 1)
                    elif kind == "O":
                        if a == 0 and k == 0:
                            dve.wait_ge(x_bias, 1)
                        residual(2 * a, k, proj_bank(k))
                        stats_of(2 * a, k)
                scale(2 * a, 0, 2 * a)
                for t in range(4, NT):
                    residual(2 * a, t, proj_bank(t))
                    stats_of(2 * a, t)
                    if t == 5:
                        second_part(0, 2 * a)
                scale(2 * a, 1, 2 * a)

            def ffn(a):
                n = 2 * a + 1
                for k in range(12):
                    dve.wait_ge(gate_done, 12 * a + k + 1)
                    if k >= 2:
                        dve.wait_ge(h_lo_done, 12 * a + k - 1)
                    dve.scalar_tensor_tensor(out=hid[:, k % 2, :], in0=ring[:, GU_SLOT[k], 1, :],
                                             scalar=DEQUANT * DEQUANT, in1=gate[:, k % 2, :],
                                             op0=ALU.mult, op1=ALU.mult).then_inc(hid_done, 1)
                    if k == 1:
                        second_part(1, 2 * a)
                    if k >= 9:
                        residual(n, k - 9, opsum[:, (k - 9) % 2, :])
                        if a == 0:
                            stats_of(n, k - 9)
                    if a == 1 and k >= 8:
                        if k == 8:
                            dve.wait_ge(x_in, 16)
                        stats_of(n, 2 * (k - 8))
                        stats_of(n, 2 * (k - 8) + 1)
                residual(n, 3, opsum[:, 1, :])
                if a == 0:
                    stats_of(n, 3)
                scale(n, 0, n)
                residual(n, 4, opsum[:, 0, :])
                if a == 0:
                    stats_of(n, 4)
                    second_part(0, n)
                    for t in range(5, NT):
                        residual(n, t, opsum[:, t % 2, :])
                        stats_of(n, t)
                    scale(n, 1, n)
                else:
                    second_part(0, n)
                    scale(n, 1, n)
                    residual(n, 5, opsum[:, 1, :])
                    second_part(1, n)
                    for t in range(6, NT):
                        residual(n, t, opsum[:, t % 2, :])

            def stats_first():
                dve.wait_ge(x_in, 16)
                for t in range(NT):
                    dve.bn_stats(stats[:, t, :], x_next[:, t, :]).then_inc(stats_done, 1)
                    dve.wait_ge(stats_done, t + 1)
                    dve.bn_aggr(mv[:, t, :], stats[:, t, :]).then_inc(aggr_done, 1)

            stats_first()
            for n, (_, _, ints) in enumerate(weights):
                dve.wait_ge(s_raw[n], 16)
                if ints:
                    dve.tensor_copy(raw[n][:], raw_i[n][:]).then_inc(s_split, 1)
                else:
                    dve.engine_nop().then_inc(s_split, 1)
                src, hi, lo = split_at(n)
                dve.wait_ge(s_first, n + 1)
                if n >= 2:
                    dve.wait_ge(s_img[n % 2], stored_before(n))
                    dve.wait_ge(s_wide, 1)
                dve.tensor_tensor(lo, src, hi.bitcast(F32), ALU.subtract).then_inc(s_split, 1)
                if n == 0:
                    scale(3, 0, 0)
                    dve.wait_ge(s_small, 16 * 6)
                    dve.tensor_copy(bv_all[:], bv_col[:, :, None].to_broadcast([P, 2, P])).then_inc(s_bias, 1)
                elif n == 1:
                    second_part(0, 0)
                    scale(3, 1, 0)
                elif n == 2:
                    second_part(1, 0)
            dve.wait_ge(s_wide, 1)
            dve.tensor_reduce(second[:, 0:1], opsum[:, 0, 0:P], AX.X, ALU.max).then_inc(s_wide, 1)
            dve.wait_ge(s_wide, 3)
            dve.tensor_reduce(second[0:1, 1:2], opsum[0:1, 1, 0:P], AX.X, ALU.max).then_inc(s_wide, 1)
            dve.wait_ge(s_wide, 4)
            dve.tensor_scalar(wide[:], second[0:1, 1:2], 0.0, None, ALU.is_gt).then_inc(s_wide, 1)
            dve.wait_ge(s_wide, 5)
            dve.wait_ge(s_pool, 15)
            dve.tensor_copy(ident_b[:], ident[:]).then_inc(s_split, 1)
            dve.tensor_copy(mask_a[0][:], mask_f[:, 0, 0:P]).then_inc(s_split, 1)
            dve.tensor_copy(mask_a[1][:], mask_f[:, 1, :]).then_inc(s_split, 1)
            dve.tensor_copy(mask_b[:], mask_f[:, 2, :]).then_inc(s_split, 1)
            for m in range(4):
                dve.tensor_scalar(bias_q4[:, m:m + 1], bias_qk[:, m:m + 1], (QSCALE, 1.0)[m % 2], None,
                                  ALU.mult).then_inc(s_split, 1)
            done = 2 * len(weights) + 8
            dve.tensor_copy(k_pre[:, :, 0, :], k_raw[:]).then_inc(s_split, 1)
            for n in range(2):
                dve.wait_ge(s_split, done + 1)
                src = k_raw[:] if n == 0 else k_res[:, :, 0, :]
                dve.tensor_tensor(k_res[:, :, n, :], src, k_pre[:, :, n, :], ALU.subtract).then_inc(s_split, 1)
                dve.wait_ge(s_split, done + 2)
                dve.tensor_copy(k_pre[:, :, n + 1, :], k_res[:, :, n, :]).then_inc(s_split, 1)
                done += 2
            dve.wait_ge(s_split, done + 1)
            dve.wait_ge(s_bias, 2)
            dve.tensor_tensor(bias_p[:], bias_p[:], ring[:, 2, 0, 0:E], ALU.add).then_inc(s_bias, 1)
            dve.wait_ge(s_bias, 3)
            for i in range(2):
                dve.wait_ge(s_img[i], 64 * (3, 2)[i])
            dve.wait_ge(s_ones, 32)
            dve.engine_nop().then_inc(s_dve, 1)

            end_batch(dve, go_on["dve"])

            with dve.Fori(0, B):
                for a in range(2):
                    attention(a)
                    ffn(a)
                end_batch(dve, go_on["dve"])

        @block.scalar
        def _(act):
            def first_of_weights(n):
                act.wait_ge(s_raw[n], 16)
                act.wait_ge(s_split, 2 * n + 1)
                if n >= 2:
                    act.wait_ge(s_img[n % 2], stored_before(n))
                src, hi, _ = split_at(n)
                act.activation(hi, src, ACT.Copy).then_inc(s_first, 1)

            def root(h, base):
                act.wait_ge(aggr_done, NT * base + 4 * h + 4)
                act.activation(std[:, 4 * h:4 * h + 4], mv[:, 4 * h:4 * h + 4, 1], ACT.Sqrt,
                               bias=EPS).then_inc(std_done, 1)

            def first_of_turned(h, base):
                act.wait_ge(turned, 2 * base + h + 1)
                act.activation(xt_hi[:, :, cols(h)], ring[:, h, :, :], ACT.Copy).then_inc(xhi_done, 1)

            def load_table(function, n):
                act.activation(table[:, n:n + 1], table[:, 8:9], function).then_inc(table_in, 1)

            def value(a, t):
                act.wait_ge(v_ready, VT_BASE[a] + t + 1)
                rows = slice(W if a == 1 and t == 0 else 0, P)
                if a == 1 and t == 0:
                    act.activation(V[0:W, 0, :, :, 0], v_pre[:].rearrange("p (h d) -> p h d", d=DH),
                                   ACT.Copy).then_inc(v_half, 1)
                act.activation(V[rows, t, :, :, 0],
                               opsum[rows, t % 2, 0:E].rearrange("p (h d) -> p h d", d=DH),
                               ACT.Copy).then_inc(v_half, 1)

            def attention(a):
                plan = PLANS[a]
                for e in plan.events:
                    kind, g, k = e
                    if kind == "P":
                        value(a, k)
                    elif kind == "Q":
                        for which in range(2):
                            n = 8 * a + 4 * g + 2 * k + which
                            m = 2 * g + which
                            act.wait_ge(qk_ready, n + 1)
                            if n >= 2:
                                act.wait_ge(part_rest, n - 1)
                                act.wait_ge(part_hi, n - 1)
                            act.activation(t32[:, n % 2, :], ring[:, plan.slot[e], which, :], ACT.Identity,
                                           bias=bias_q4[:, m:m + 1] if a == 0 else 0.0,
                                           scale=(QSCALE, 1.0)[which]).then_inc(qk_evac, 1)
                            act.wait_ge(qk_evac, n + 1)
                            act.activation(part_of(n - 8 * a)[:, 0, :], t32[:, n % 2, :],
                                           ACT.Copy).then_inc(part_hi, 1)
                        if a == 1 and (g, k) == (0, 0):
                            first_of_turned(1, 1)
                        if (g, k) == (1, 1):
                            load_table(ACT.Exp, 4 * a)
                    elif kind == "B":
                        jt, h, heads, _ = unit = plan.b_units[k]
                        j = g * plan.n_j + jt
                        if k == 0 and g == 0:
                            for s in stack_in:
                                act.wait_ge(s, 192 * (a + 1))
                        act.wait_ge(b_ready, B_BASE[a] + g * plan.n_b + k + 1)
                        if j >= 2:
                            act.wait_ge(pv_done, V_BASE[a] + j - 1)
                        w = plan.b_width(jt)
                        act.activation(probs[:, j % 2, h:h + heads, 0:w], heads_of(plan.slot[e], unit, w),
                                       ACT.Exp).then_inc(exp_done, 1)
                    elif kind == "C":
                        act.wait_ge(pv_done, V_BASE[a] + plan.n_j * g + plan.last[k] + 1)
                        if g:
                            act.wait_ge(on_f, NORMED * a + plan.nth["M", g - 1, k] + 1)
                        elif a == 0:
                            act.wait_ge(x_bias, 2)
                        else:
                            act.wait_ge(packed[k], 128)
                        act.activation(osb[:, k, :], opsum[:, k, :], ACT.Copy).then_inc(o_copied, 1)
                    elif kind == "H":
                        mult = ("D" if g == GROUPS - 1 else "M", g, k)
                        act.wait_ge(on_f, NORMED * a + plan.nth[mult] + 1)
                        if 4 * a + g:
                            act.wait_ge(packed[k], 32 * (4 * a + g))
                        act.activation(o_hi[:, k, :], normed(g)[:, k, :], ACT.Copy).then_inc(on_hi_done, 1)
                load_table(ACT.Sqrt, 4 * a + 1)
                root(0, 2 * a)
                first_of_turned(0, 2 * a)
                root(1, 2 * a)
                load_table(ACT.Silu, 4 * a + 2)

            def ffn(a):
                n = 2 * a + 1

                def first_part(k):
                    n, m = divmod(k, M_HID)
                    act.wait_ge(hid_done, 12 * a + k + 1)
                    act.activation(h_hi[:, m, HALF * n:HALF * n + HALF], hid[:, k % 2, :],
                                   ACT.Copy).then_inc(h_hi_done, 1)

                for k in range(12):
                    if k == 2:
                        first_of_turned(1, 2 * a)
                    act.wait_ge(gu_ready, 12 * a + k + 1)
                    if k >= 2:
                        act.wait_ge(hid_done, 12 * a + k - 1)
                    act.activation(gate[:, k % 2, :], ring[:, GU_SLOT[k], 0, :], ACT.Silu,
                                   scale=DEQUANT).then_inc(gate_done, 1)
                    if k:
                        first_part(k - 1)
                first_part(11)
                load_table(ACT.Sqrt, 4 * a + 3)
                root(0, n)
                first_of_turned(0, n)
                root(1, n)
                if a == 1:
                    first_of_turned(1, n)

            root(0, 0)
            root(1, 0)
            for n in range(len(weights)):
                first_of_weights(n)
                if n in (0, 1):
                    first_of_turned(n, 0)
            end_batch(act, go_on["act"])

            with act.Fori(0, B):
                for a in range(2):
                    attention(a)
                    ffn(a)
                end_batch(act, go_on["act"])

        @block.tensor
        def _(pe):
            def turn(h, base):
                for tt in range(4):
                    pe.wait_ge(xn_done, NT * base + 4 * h + tt + 1)
                    for k in range(2):
                        last = pe.transpose(ring[:, h, k, P * tt:P * tt + P], xn[:, tt, P * k:P * k + P],
                                            ident[:])
                last.then_inc(turned, 1)

            def qk(a, e):
                _, p, n = e
                if a == 1:
                    pe.wait_ge(xlo_done, 2 + n + 1)
                for which in range(2):
                    m = 2 * p + which
                    dst = ring[:, PLANS[a].slot[e], which, :]
                    for k in range(2):
                        hi = w_qkv[:, 512 * k + P * m:512 * k + P * m + P]
                        lo = w_qkv[:, 1024 + 512 * k + P * m:1024 + 512 * k + P * m + P]
                        pe.matmul(dst, hi, xt_hi[:, k, cols(n)], start=(k == 0), stop=False)
                        pe.matmul(dst, hi, xt_lo[:, k, cols(n)], start=False, stop=False)
                        last = pe.matmul(dst, lo, xt_hi[:, k, cols(n)], start=False, stop=(k == 1))
                    last.then_inc(qk_ready, 1)

            def value(a, t):
                c = P * t + (W if a == 0 else 0)
                if t >= 2:
                    pe.wait_ge(v_done, VT_BASE[a] + t - 1)
                dst = opsum[:, t % 2, :]
                for k in range(2):
                    wv = w_qkv[:, 2048 + 512 * k:2048 + 512 * k + 512]
                    pe.matmul(dst, xt_hi[:, k, c:c + P], wv, start=(k == 0), stop=False)
                    last = pe.matmul(dst[:, 0:E], xt_lo[:, k, c:c + P], wv[:, 0:E], start=False, stop=(k == 1))
                last.then_inc(v_ready, 1)

            def project(a, t):
                if t % 4 == 0:
                    pe.wait_ge(packed[t // 4], 128 * (a + 1))
                if t == 0:
                    pe.wait_ge(wp_in, 16 * (a + 1))
                if t >= 3:
                    pe.wait_ge(res_done, 2 * NT * a + t - 2)
                dst = proj_bank(t)
                for k in range(2):
                    pe.matmul(dst, on_hi[:, k, P * t:P * t + P], wp_sb[:, k, :], start=(k == 0), stop=False)
                    last = pe.matmul(dst[:, 0:E], on_lo[:, k, P * t:P * t + P], wp_sb[:, k, 0:E],
                                     start=False, stop=(k == 1))
                last.then_inc(proj_ready, 1)

            def attention(a):
                plan = PLANS[a]
                if a == 1:
                    pe.wait_ge(qkv_in, 16)

                released = {"A": (a_max, A_BASE[a], plan.n_a), "B": (exp_done, B_BASE[a], plan.n_b),
                            "T": (peak_done, 4 * a, 1)}

                def slot_free(e):
                    if plan.before[e]:
                        kind, g, k = plan.before[e]
                        if kind == "Q":
                            pe.wait_ge(qk_evac, 8 * a + 4 * g + 2 * k + 2)
                        else:
                            s, base, per = released[kind]
                            pe.wait_ge(s, base + g * per + k + 1)

                def masks(slot, unit, width, mask):
                    _, _, heads, per = unit
                    w = mask.shape[-1]
                    together = 2 if per == 256 else 1
                    for n in range(0, heads, together):
                        dst = flat(slot)[:, per * n:per * (n + together)]
                        dst = dst.rearrange("p (h c) -> p h c", h=together)[:, :, width - w:width]
                        last = pe.matmul(dst, ident_b[:], mask[:, None, :].to_broadcast([P, together, w]),
                                         start=False, stop=True, skip_group_check=True)
                    return last

                for e in plan.events:
                    kind, g, k = e
                    if kind == "P":
                        value(a, k)
                    elif kind == "Q":
                        if a == 1 and (g, k) == (0, 0):
                            pe.wait_ge(hid_done, 10)
                        slot_free(e)
                        qk(a, e)
                        if a == 1 and (g, k) == (0, 0):
                            turn(1, 1)
                    elif kind == "A":
                        i, h0, heads, per = unit = plan.a_units[k]
                        if g == 0 and k == 0:
                            pe.wait_ge(stack_in[0], 192 * (a + 1))
                        if g == 0 and i == 4 and h0 == 0:
                            pe.wait_ge(stack_in[1], 192 * (a + 1))
                        if g == 2 and k == 0:
                            pe.wait_ge(stack_in[2], 192 * (a + 1))
                        slot_free(e)
                        w = plan.a_width(i)
                        first_key = W if a == 0 else P * i
                        for n in range(heads):
                            q = q_st[0:SP_ROWS, HG * g + h0 + n, P * i:P * i + P]
                            for c in range(0, w, 512):
                                d = min(512, w - c)
                                pe.matmul(flat(plan.slot[e])[:, per * n + c:per * n + c + d], q,
                                          k_st[0:SP_ROWS, HG * g + h0 + n, first_key + c:first_key + c + d],
                                          start=(per * n % 512 == 0), stop=False, skip_group_check=True)
                        masks(plan.slot[e], unit, w, mask_a[a][:]).then_inc(a_ready, 1)
                    elif kind == "T":
                        slot_free(e)
                        pe.wait_ge(a_max, A_BASE[a] + plan.n_a * (g + 1))
                        pe.transpose(ring[0:32, plan.slot[e], 0, 0:P], peak[:, g % 2, :],
                                     ident[:]).then_inc(t_ready, 1)
                    elif kind == "B":
                        if k == 0:
                            pe.wait_ge(peak_rows, 32 * (4 * a + g + 1))
                            if g == 0:
                                pe.wait_ge(ones_in, 16 * (a + 1))
                        slot_free(e)
                        j, h0, heads, per = unit = plan.b_units[k]
                        q0, q1 = plan.queries(j)
                        w = q1 - q0
                        first_key = P * j + (W if a == 0 else 0)
                        for n in range(heads):
                            kk = k_st[:, HG * g + h0 + n, first_key:first_key + P]
                            for c in range(0, w, 512):
                                d = min(512, w - c)
                                last = pe.matmul(flat(plan.slot[e])[:, per * n + c:per * n + c + d], kk,
                                                 q_st[:, HG * g + h0 + n, q0 + c:q0 + c + d],
                                                 start=(per * n % 512 == 0), stop=(a == 0),
                                                 skip_group_check=True)
                        if a == 1:
                            first = q0 - (P * j - W)
                            last = masks(plan.slot[e], unit, w, mask_b[:, first:first + w])
                        last.then_inc(b_ready, 1)
                    elif kind == "V":
                        jj = g * plan.n_j + k
                        if a == 0:
                            pe.wait_ge(masked, jj + 1)
                        else:
                            pe.wait_ge(exp_done, B_BASE[a] + g * plan.n_b + plan.b_upto[k])
                        if k == 0 and g == 0:
                            pe.wait_ge(v_done, VT_BASE[a] + VT[a])
                            if a == 1:
                                pe.wait_ge(v_half, VT_BASE[a] + 1)
                        q0, q1 = plan.queries(k)
                        for bank in range(2):
                            c0, c1 = max(q0, 512 * bank), min(q1, 512 * bank + 512)
                            if c0 >= c1:
                                continue
                            opens, closes = k == plan.opens[bank], k == plan.last[bank]
                            if opens and g > 0:
                                pe.wait_ge(o_copied, COPIED * a + 2 * (g - 1) + bank + 1)
                            for h in range(HG):
                                last = pe.matmul(opsum[32 * h:32 * h + 32, bank, c0 - 512 * bank:c1 - 512 * bank],
                                                 V[:, k, HG * g + h, :, :].rearrange("p d o -> p (d o)"),
                                                 probs[:, jj % 2, h, c0 - q0:c1 - q0],
                                                 start=opens, stop=closes, skip_group_check=True)
                        last.then_inc(pv_done, 1)
                    elif kind == "O":
                        project(a, k)
                for t in range(4, NT):
                    project(a, t)
                    if t == 5:
                        turn(0, 2 * a)

            def ffn(a, wide_weights):
                n = 2 * a + 1

                def gate_up(k):
                    h, m = divmod(k, M_HID)
                    pe.wait_ge(xlo_done, 4 * a + h + 1)
                    before = [n for n in range(k) if GU_SLOT[n] == GU_SLOT[k]]
                    if before:
                        pe.wait_ge(hid_done, 12 * a + before[-1] + 1)
                    elif GU_SLOT[k] == 2:
                        pe.wait_ge(res_done, 2 * NT * a + NT)
                    elif GU_SLOT[k] == 1:
                        pe.wait_ge(xlo_done, 4 * a + 2)
                    for u in range(2):
                        dst = ring[:, GU_SLOT[k], u, :]
                        f = HIDDEN * u + P * m
                        for kk in range(2):
                            hi, lo = w_gu_sb[:, 0, kk, f:f + P], w_gu_sb[:, 1, kk, f:f + P]
                            pe.matmul(dst, hi, xt_hi[:, kk, cols(h)], start=(kk == 0), stop=False)
                            last = pe.matmul(dst, hi, xt_lo[:, kk, cols(h)], start=False,
                                             stop=(kk == 1 and not wide_weights))
                            if wide_weights:
                                last = pe.matmul(dst, lo, xt_hi[:, kk, cols(h)], start=False, stop=(kk == 1))
                    last.then_inc(gu_ready, 1)

                def down(t):
                    pe.wait_ge(h_lo_done, 12 * a + M_HID * (t // 4 + 1))
                    if t >= 2:
                        pe.wait_ge(res_done, NT * n + t - 1)
                    dst = opsum[:, t % 2, :]
                    for m in range(M_HID):
                        pe.matmul(dst, h_hi[:, m, P * t:P * t + P], w_dn_sb[:, m, :], start=(m == 0), stop=False)
                        last = pe.matmul(dst[:, 0:E], h_lo[:, m, P * t:P * t + P], w_dn_sb[:, m, 0:E],
                                         start=False, stop=(m == M_HID - 1))
                    last.then_inc(proj_ready, 1)

                pe.wait_ge(gu_in, 32 * (a + 1))
                for k in range(12):
                    gate_up(k)
                    if k == 1:
                        turn(1, 2 * a)
                    if k >= 9:
                        down(k - 9)
                down(3)
                for t in range(4, NT):
                    down(t)
                    if t == 4:
                        pe.wait_ge(hid_done, 12 * a + 12)
                        turn(0, n)
                    if t == 5 and a == 1:
                        turn(1, n)

            pe.wait_ge(s_pool, 3)
            for h in range(2):
                turn(h, 0)
            pe.wait_ge(s_split, 2)
            for k in range(4 * HIDDEN // P):
                lo = st_lo[0][:, P * k:P * k + P]
                last = pe.matmul(opsum[:, 0, 0:P], lo, lo, start=(k == 0), stop=(k == 4 * HIDDEN // P - 1))
            last.then_inc(s_wide, 1)
            pe.wait_ge(s_raw[4], 16)
            pe.wait_ge(s_bias, 1)
            for k in range(2):
                last = pe.matmul(ring[:, 2, 0, 0:E], bv_all[:, k, :], raw[4][:, E * k:E * k + E],
                                 start=(k == 0), stop=(k == 1))
            last.then_inc(s_bias, 1)
            pe.wait_ge(s_wide, 2)
            pe.transpose(opsum[0:1, 1, 0:P], second[:, 0:1], ident[:]).then_inc(s_wide, 1)
            pe.wait_ge(s_wide, 5)
            end_batch(pe, go_on["pe"])

            has_second = pe.value_load(wide[0:1, 0:1], min_val=0, max_val=1)
            with pe.Fori(0, B):
                for a in range(2):
                    attention(a)
                    with pe.If(has_second > 0):
                        ffn(a, True)
                    with pe.Else():
                        ffn(a, False)
                end_batch(pe, go_on["pe"])

        @block.sync
        def _(sp):
            x_rows = x.rearrange("b (t p) e -> b p t e", p=P)
            out_rows = out.rearrange("b (t p) e -> b p t e", p=P)
            def load(n):
                src, _, ints = weights[n]
                sp.dma_start((raw_i if ints else raw)[n][:], src).then_inc(s_raw[n], 16)

            sp.dma_start(x_next[:], x_rows[0]).then_inc(x_in, 16)
            load(0)
            load(1)
            for dst, src in ((bias_qk[:], b_qk), (bv_col[:], b_v),
                             (bias_p[:], b_p.partition_broadcast(P)), (v_pre[:], v_init),
                             (k_raw[:, 0, :], k_init[0:P, :]), (k_raw[:, 1, :], k_init[P:2 * P, :])):
                sp.dma_start(dst, src).then_inc(s_small, 16)
            for n in range(2, len(weights)):
                load(n)

            def store(n):
                i = n % 2
                sp.wait_ge(s_split, 2 * n + 2)
                hi, lo = st_hi[i][:].bitcast(F32), st_lo[i][:].bitcast(F32)
                if n in (1, 2):
                    qk = img_qkv[n - 1][:, 0:2048].rearrange("p (s k c) -> p s k c", s=2, k=2)
                    v = img_qkv[n - 1][:, 2048:3072].rearrange("p (k s c) -> p s k c", s=2, k=2)
                    for s, t in enumerate((hi, lo)):
                        src = t[:, 0:1536].rearrange("p (k c) -> p k c", k=2)
                        sp.dma_start(qk[:, s], src[:, :, 0:512]).then_inc(s_img[i], 16)
                        sp.dma_start(v[:, s], src[:, :, 512:768]).then_inc(s_img[i], 16)
                elif n in (4, 5):
                    dst = img_wp[n - 4].rearrange("p (g s c) -> p s g c", g=2, s=2)
                    for s, t in enumerate((hi, lo)):
                        src = t[:, 0:512].rearrange("p (g c) -> p g c", g=2)
                        for k in range(2):
                            sp.dma_start(dst[:, s, k], src[:, k]).then_inc(s_img[i], 16)
                elif n == 0:
                    for s, t in enumerate((hi, lo)):
                        for k in range(2):
                            c = slice(1536 * k, 1536 * k + 1536)
                            sp.dma_start(img_gu[:, 3072 * s + 1536 * k:3072 * s + 1536 * k + 1536],
                                         t[:, c]).then_inc(s_img[i], 16)

            sp.wait_ge(s_pool, 10)
            for r in range(2):
                sp.dma_start(ones_dram[r:r + 1, :].rearrange("o (a c) -> (o a) c", c=288),
                             ones_b[0:64, :, :].rearrange("p a c -> p (a c)")).then_inc(s_ones, 8 * 2)
            def load_qkv(a):
                sp.dma_start(w_qkv[:].bitcast(F32), img_qkv[a]).then_inc(qkv_in, 16)

            for n in range(3):
                store(n)
            sp.wait_ge(s_img[1], 64)
            load_qkv(0)
            for n in (4, 5):
                store(n)
            sp.wait_ge(s_ones, 32)
            sp.wait_ge(s_dve, 1)

            late = (stats_done, aggr_done, std_done, rstd_done, xn_done, turned, xhi_done, xlo_done,
                    proj_ready, res_half, res_done)

            def next_batch(reached):
                for s, n in reached.items():
                    sp.wait_ge(s, n)
                sp.wait_ge(arrived, 4)
                sp.sem_clear(counted)
                sp.sem_clear(arrived)
                for go in go_on.values():
                    sp.sem_inc(go, 1)

            def load_gu(a, part, groups):
                sp.wait_ge(b_ready, B_BASE[a] + groups * PLANS[a].n_b)
                sp.dma_start(w_gu_sb[:, part, :, :].rearrange("p k c -> p (k c)").bitcast(F32),
                             img_gu[:, 3072 * part:3072 * part + 3072]).then_inc(gu_in, 16)

            def attention(a):
                plan = PLANS[a]
                if a == 1:
                    sp.wait_ge(proj_ready, 2 * NT)
                sp.dma_start(k_st[SP_ROWS:MAX_ROWS, :, :].rearrange("p h c -> p (h c)"),
                             ones_dram).then_inc(ones_in, 16)
                if a == 1:
                    sp.wait_ge(kpads, 2)

                def stack(which, heads, half, part):
                    n = 8 * a + 4 * heads + 2 * (1 if half is None else half) + which
                    sp.wait_ge((part_hi, part_mid, part_lo)[part], n + 1)
                    lo, hi = (0, S) if half is None else (HALF * half, HALF * half + HALF)
                    at_heads = slice(8 * heads, 8 * heads + 8)
                    for blk in range(6):
                        if (Q_PART, K_PART)[which][blk] != part:
                            continue
                        rows = slice(DH * blk, DH * blk + DH)
                        if which == 0:
                            dst, src = q_st[rows, at_heads, lo:hi], q_part[:, heads, part, lo:hi]
                        else:
                            c = slice(W + lo - (W if a == 1 and lo == 0 else 0),
                                      W + hi + (W if a == 1 and hi == S else 0))
                            dst, src = k_st[rows, at_heads, c], k_part[:, heads, part, c]
                        sp.dma_start(dst, src).then_inc(stack_in[2 if heads else half], 16)

                for heads, half in ((0, 0), (0, 1), (1, None)):
                    for which, part in ((0, 0), (0, 1), (1, 0), (0, 2), (1, 1), (1, 2)):
                        stack(which, heads, half, part)
                sp.dma_start(wp_sb[:].rearrange("p g c -> p (g c)").bitcast(F32), img_wp[a]).then_inc(wp_in, 16)

                for e in plan.events:
                    kind, g, k = e
                    if kind == "T":
                        sp.wait_ge(peak_done, 4 * a + g + 1)
                        for r in range(2):
                            sp.dma_start(q_st[SP_ROWS + r:SP_ROWS + r + 1, HG * g:HG * g + HG, :],
                                         peak_b[:, r, :]).then_inc(peak_rows, 16)
                    elif kind == "C":
                        sp.wait_ge(o_copied, COPIED * a + plan.nth[e] + 1)
                        sp.dma_start(sums[:, k, :], osb[1:P:32, k, :]).then_inc(sums_out[k], 16)
                    elif kind == "R":
                        sp.wait_ge(rsum_done, COPIED * a + plan.nth[e] + 1)
                        if 4 * a + g:
                            sp.wait_ge(packed[k], 32 * (4 * a + g))
                        sp.dma_start(onf[0:P:32, k, :], rsum[:, k, :]).then_inc(rsum_back[k], 16)
                    elif kind == "K":
                        sp.wait_ge(on_lo_done, NORMED * a + plan.nth["H", g, k] + 1)
                        rows = slice(64 * (g % 2), 64 * (g % 2) + 64)
                        c = slice(HALF * k, HALF * k + HALF)
                        for dst, src in ((on_hi, o_hi), (on_lo, normed(g))):
                            sp.dma_start(dst[rows, g // 2, c].bitcast(F32),
                                         src[0:P:2, k, :].bitcast(F32)).then_inc(packed[k], 16)
                    elif e == ("B", 2, 1):
                        load_gu(a, 0, 2)
                    elif e == ("B", 3, 1) and a == 0:
                        load_gu(a, 1, 3)
                if a == 1:
                    load_gu(a, 1, 3)

            next_batch(first)
            sp.sem_inc(out_stored, 32)
            with sp.Fori(0, B) as b:
                sp.wait_ge(out_stored, 32)
                sp.sem_clear(out_stored)
                sp.sem_inc(x_free, 1)
                for a in range(2):
                    attention(a)
                    if a == 1:
                        for k in range(2):
                            sp.wait_ge(packed[k], 256)
                        sp.dma_start(x_next[:], x_rows[(b + 1) % B]).then_inc(x_in, 16)
                    sp.wait_ge(proj_ready, 2 * NT * a + NT)
                    load_qkv(1 - a)
                for s, n in totals.items():
                    if s not in late:
                        sp.wait_ge(s, n)
                sp.wait_ge(res_done, 3 * NT + 4)
                sp.dma_start(out_rows[b, :, 0:4], X[:, 0:4, :]).then_inc(out_stored, 16)
                next_batch({s: totals[s] for s in late})
                sp.dma_start(out_rows[b, :, 4:NT], X[:, 4:NT, :]).then_inc(out_stored, 16)
            sp.wait_ge(out_stored, 32)


def kernel(L0_attn_a_x, L0_attn_a_W1, L0_attn_a_b1, L0_attn_a_Wp, L0_attn_a_bp, L0_attn_b_Wq, L0_attn_b_Wk,
           L0_attn_b_Wv, L0_attn_b_Wo, L0_attn_b_last_k_init, L0_attn_b_last_v_init, L0_ffn_w_gate, L0_ffn_w_up,
           L0_ffn_w_down):
    import concourse.bacc as bacc
    from concourse.bass_utils import run_bass_kernel_spmd

    def halves(w):
        w = np.asarray(w).reshape(-1, 2, 8, DH).transpose(0, 1, 3, 2)
        return w.reshape(w.shape[0], 2, P)

    def rows(w):
        w = np.asarray(w)
        return np.ascontiguousarray(w.reshape(-1, P, w.shape[1]).transpose(1, 0, 2).reshape(P, -1))

    def qkv(q, k, v):
        q, k = halves(q), halves(k)
        qk = np.stack([q, k], axis=2).reshape(q.shape[0], 4 * P)
        return rows(np.concatenate([qk, np.asarray(v)], axis=1))

    w1 = np.asarray(L0_attn_a_W1).reshape(E, HEADS, 3, DH)
    b1 = np.asarray(L0_attn_a_b1).reshape(1, HEADS, 3, DH)
    q1, k1, v1 = (w1[:, :, i].reshape(E, E) for i in range(3))
    bq, bk, bv = (b1[:, :, i].reshape(1, E) for i in range(3))
    b_qk = np.ascontiguousarray(np.stack([halves(bq)[0], halves(bk)[0]], axis=1).reshape(4, P).T)
    last_k = np.asarray(L0_attn_b_last_k_init)
    last_v = np.asarray(L0_attn_b_last_v_init).reshape(W - 1, E)
    kt = halves(last_k.reshape(W - 1, E)).reshape(W - 1, E).T
    data = {
        "x": np.asarray(L0_attn_a_x),
        "att_a": qkv(q1, k1, v1),
        "att_b": qkv(np.asarray(L0_attn_b_Wq).T, np.asarray(L0_attn_b_Wk).T, np.asarray(L0_attn_b_Wv).T),
        "b_qk": b_qk,
        "b_v": np.ascontiguousarray(bv.reshape(2, P).T),
        "wp_a": rows(L0_attn_a_Wp),
        "wp_b": rows(np.asarray(L0_attn_b_Wo).T),
        "b_p": np.asarray(L0_attn_a_bp),
        "w_gu": rows(np.concatenate([np.asarray(L0_ffn_w_gate).T, np.asarray(L0_ffn_w_up).T], axis=1)),
        "w_dn": rows(np.asarray(L0_ffn_w_down).T),
        "k_init": np.ascontiguousarray(np.concatenate([np.zeros_like(kt[:, :1]), kt], axis=1)),
        "v_init": np.concatenate([np.zeros_like(last_v[:1]), last_v], axis=0),
    }
    nc = bacc.Bacc("TRN2", target_bir_lowering=False, num_devices=1)
    arrays, args = {}, []
    for name, a in data.items():
        a = np.ascontiguousarray(a)
        arrays[f"in_{name}"] = a
        args.append(nc.dram_tensor(f"in_{name}", a.shape, mybir.dt.from_np(a.dtype), kind="ExternalInput").ap())
    args.append(nc.dram_tensor("y", (B, S, E), F32, kind="ExternalOutput").ap())
    layers_kernel(nc, *args)
    got = run_bass_kernel_spmd(nc, [arrays], core_ids=[0])
    return got.results[0]["y"]
```
